# Optimizing a Trainium2 kernel written in Bass

```python
import numpy as np
import jax
import jax.numpy as jnp

def _softmax(x, axis=-1):
    return jax.nn.softmax(x, axis=axis)

def _gelu(x):
    return jax.nn.gelu(x, approximate=True)

def _silu(x):
    return jax.nn.silu(x)

def _sigmoid(x):
    return jax.nn.sigmoid(x)

def _layernorm(x, axis=-1, eps=1e-05):
    m = jnp.mean(x, axis=axis, keepdims=True)
    v = jnp.var(x, axis=axis, keepdims=True)
    return (x - m) / jnp.sqrt(v + eps)

def _scatter_add(tgt, idx, src, axis=0):
    return tgt.at[idx].add(src)

def _segment_sum(src, seg, n):
    return jax.ops.segment_sum(src, seg, n)
kernel_name = 'mk_adaln_ffn_d2_seqx_r8_55b6e7'

def setup_inputs(seed: int=0):
    np.random.seed(seed)
    _w = jnp.asarray

    def _rec_inputs():
        import jax
        import jax.numpy as jnp
        _rk = jax.random.key(seed)
        x = 7.22e-05 + 1 * jax.random.normal(jax.random.fold_in(_rk, 1), (128, 32, 512), jnp.float32)
        _lenS = 32 - jax.random.randint(jax.random.fold_in(_rk, 7), (128,), 0, max(1, 32 // 4) + 1, jnp.int32)
        _lenS2 = 32 - jax.random.randint(jax.random.fold_in(_rk, 8), (128,), 0, max(1, 32 // 4) + 1, jnp.int32)
        itok_B_2_6 = jax.random.randint(jax.random.fold_in(_rk, 11), (128,), 2, 7, jnp.int32)
        itok_B_4_50 = jax.random.randint(jax.random.fold_in(_rk, 12), (128,), 4, 51, jnp.int32)
        return (x, itok_B_2_6, itok_B_4_50)
    x, itok_B_2_6, itok_B_4_50 = _rec_inputs()

    def _L0_cond_setup():
        import jax, jax.numpy as jnp
        import numpy as np
        B, N, H, F = (4, 64, 512, 1376)
        L, R, RANK = (1, 16, 16)
        SCALE = 0.5
        key = jax.random.key(seed)
        ks = jax.random.split(key, 12)
        nrm = lambda k, shape, fan: jax.random.normal(k, shape, jnp.float32) * fan ** (-0.5)
        inp = {'x': jax.random.normal(ks[0], (B, N, H), jnp.float32), 'W_gate': nrm(ks[1], (F, H), H), 'W_up': nrm(ks[2], (F, H), H), 'W_down': nrm(ks[3], (H, F), F), 'A_gate': nrm(ks[4], (L, R, RANK, H), H), 'B_gate': nrm(ks[5], (L, R, F, RANK), RANK), 'A_up': nrm(ks[6], (L, R, RANK, H), H), 'B_up': nrm(ks[7], (L, R, F, RANK), RANK), 'A_down': nrm(ks[8], (L, R, RANK, F), F), 'B_down': nrm(ks[9], (L, R, H, RANK), RANK), 'lora_indices': jax.random.randint(ks[10], (B,), 0, R), 'layer_idx': 0}
        return inp
    _L0_cond_all = _L0_cond_setup()
    _L0_cond_in = {k: v for k, v in _L0_cond_all.items() if k in ('W_gate', 'W_up', 'W_down', 'A_gate', 'B_gate', 'A_up', 'B_up', 'A_down', 'B_down')}
    del _L0_cond_all

    def _L0_ffn_setup():
        import jax, jax.numpy as jnp
        import numpy as np
        key = jax.random.key(seed)
        k1, k2, k3 = jax.random.split(key, 3)
        d_in, d_out = (512, 512)
        x = jax.random.normal(k1, (8, 128, d_in), dtype=jnp.float32)
        weight = jax.random.normal(k2, (d_out, d_in), dtype=jnp.float32) * (1.0 / np.sqrt(d_in))
        bias = jax.random.uniform(k3, (d_out,), dtype=jnp.float32, minval=-1.0 / np.sqrt(d_in), maxval=1.0 / np.sqrt(d_in))
        return {'x': x, 'weight': weight, 'bias': bias}
    _L0_ffn_all = _L0_ffn_setup()
    _L0_ffn_in = {k: v for k, v in _L0_ffn_all.items() if k in ('weight', 'bias')}
    del _L0_ffn_all

    def _L1_cond_setup():
        import jax, jax.numpy as jnp
        import numpy as np
        RANK = 16
        ALPHA = 16.0
        SCALING = ALPHA / RANK
        key = jax.random.key(seed)
        k1, k2, k3, k4 = jax.random.split(key, 4)
        batch, n_tok, d_in, d_out, n_adapters, rank = (8, 256, 512, 512, 64, RANK)
        x = jax.random.normal(k1, (batch, n_tok, d_in), dtype=jnp.float32)
        A = jax.random.normal(k2, (n_adapters, d_out, rank), dtype=jnp.float32) * 0.02
        B = jax.random.normal(k3, (n_adapters, rank, d_in), dtype=jnp.float32)
        adapter_ids = jax.random.randint(k4, (batch,), 0, n_adapters, dtype=jnp.int32)
        return {'x': x, 'A': A, 'B': B, 'adapter_ids': adapter_ids}
    _L1_cond_all = _L1_cond_setup()
    _L1_cond_in = {k: v for k, v in _L1_cond_all.items() if k in ('A', 'B')}
    del _L1_cond_all

    def _L1_ffn_setup():
        import jax, jax.numpy as jnp
        import numpy as np
        B_, S, D_IN, D_OUT = (4, 256, 512, 512)
        N, RANK, ALPHA = (8, 16, 32)
        SCALE = ALPHA / RANK
        key = jax.random.key(seed)
        kx, ka, kb, kw, kbias = jax.random.split(key, 5)
        x = jax.random.normal(kx, (B_, S, D_IN), dtype=jnp.float32)
        lora_A = jax.random.normal(ka, (N, RANK, D_IN), dtype=jnp.float32) * (1.0 / np.sqrt(D_IN))
        lora_B = jax.random.normal(kb, (N, D_OUT, RANK), dtype=jnp.float32) * (1.0 / np.sqrt(RANK))
        W = jax.random.normal(kw, (D_OUT, D_IN), dtype=jnp.float32) * (1.0 / np.sqrt(D_IN))
        bias = jax.random.normal(kbias, (D_OUT,), dtype=jnp.float32) * 0.01
        lora_weights = jnp.full((N,), 1.0 / N, dtype=jnp.float32)
        return {'x': x, 'lora_A': lora_A, 'lora_B': lora_B, 'W': W, 'bias': bias, 'lora_weights': lora_weights}
    _L1_ffn_all = _L1_ffn_setup()
    _L1_ffn_in = {k: v for k, v in _L1_ffn_all.items() if k in ('lora_A', 'lora_B', 'W', 'bias', 'lora_weights')}
    del _L1_ffn_all
    return {'x': x, 'itok_B_2_6': itok_B_2_6, 'itok_B_4_50': itok_B_4_50, 'L0_cond_W_gate': _L0_cond_in['W_gate'], 'L0_cond_W_up': _L0_cond_in['W_up'], 'L0_cond_W_down': _L0_cond_in['W_down'], 'L0_cond_A_gate': _L0_cond_in['A_gate'], 'L0_cond_B_gate': _L0_cond_in['B_gate'], 'L0_cond_A_up': _L0_cond_in['A_up'], 'L0_cond_B_up': _L0_cond_in['B_up'], 'L0_cond_A_down': _L0_cond_in['A_down'], 'L0_cond_B_down': _L0_cond_in['B_down'], 'L0_ffn_weight': _L0_ffn_in['weight'], 'L0_ffn_bias': _L0_ffn_in['bias'], 'L1_cond_A': _L1_cond_in['A'], 'L1_cond_B': _L1_cond_in['B'], 'L1_ffn_lora_A': _L1_ffn_in['lora_A'], 'L1_ffn_lora_B': _L1_ffn_in['lora_B'], 'L1_ffn_W': _L1_ffn_in['W'], 'L1_ffn_bias': _L1_ffn_in['bias'], 'L1_ffn_lora_weights': _L1_ffn_in['lora_weights']}

def reference(x, itok_B_2_6, itok_B_4_50, L0_cond_W_gate, L0_cond_W_up, L0_cond_W_down, L0_cond_A_gate, L0_cond_B_gate, L0_cond_A_up, L0_cond_B_up, L0_cond_A_down, L0_cond_B_down, L0_ffn_weight, L0_ffn_bias, L1_cond_A, L1_cond_B, L1_ffn_lora_A, L1_ffn_lora_B, L1_ffn_W, L1_ffn_bias, L1_ffn_lora_weights):
    import jax
    import jax.numpy as jnp

    def _L0_cond_ref(x, W_gate, W_up, W_down, A_gate, B_gate, A_up, B_up, A_down, B_down, lora_indices, layer_idx):
        import jax, jax.numpy as jnp
        import numpy as np
        B, N, H, F = (4, 64, 512, 1376)
        L, R, RANK = (1, 16, 16)
        SCALE = 0.5

        def lora_add(base, inp, A, B):
            Ab = A[layer_idx][lora_indices]
            Bb = B[layer_idx][lora_indices]
            t = jnp.einsum('bri,bni->bnr', Ab, inp)
            return base + jnp.einsum('bor,bnr->bno', Bb, t) * SCALE
        gate = lora_add(jnp.einsum('bnh,fh->bnf', x, W_gate), x, A_gate, B_gate)
        up = lora_add(jnp.einsum('bnh,fh->bnf', x, W_up), x, A_up, B_up)
        act = jax.nn.silu(gate) * up
        down = lora_add(jnp.einsum('bnf,hf->bnh', act, W_down), act, A_down, B_down)
        return down

    def _L0_ffn_ref(x, weight, bias):
        import jax, jax.numpy as jnp
        import numpy as np
        w_bin = jnp.sign(weight)
        return jnp.einsum('bsi,oi->bso', x, w_bin) + bias

    def _L1_cond_ref(x, A, B, adapter_ids):
        import jax, jax.numpy as jnp
        import numpy as np
        RANK = 16
        ALPHA = 16.0
        SCALING = ALPHA / RANK
        B_req = B[adapter_ids]
        A_req = A[adapter_ids]
        Bx = jnp.einsum('bni,bri->bnr', x, B_req)
        out = jnp.einsum('bnr,bor->bno', Bx, A_req)
        return out * SCALING

    def _L1_ffn_ref(x, lora_A, lora_B, W, bias, lora_weights):
        import jax, jax.numpy as jnp
        import numpy as np
        B_, S, D_IN, D_OUT = (4, 256, 512, 512)
        N, RANK, ALPHA = (8, 16, 32)
        SCALE = ALPHA / RANK
        h = jnp.einsum('bsd,nrd->nbsr', x, lora_A)
        coef = (SCALE * lora_weights)[:, None, None]
        lora_out = jnp.einsum('nbsr,nor->bso', h, lora_B * coef)
        base = jnp.einsum('bsd,od->bso', x, W) + bias
        return base + lora_out
    x = x + _L0_ffn_ref(_L0_cond_ref(x, L0_cond_W_gate, L0_cond_W_up, L0_cond_W_down, L0_cond_A_gate, L0_cond_B_gate, L0_cond_A_up, L0_cond_B_up, L0_cond_A_down, L0_cond_B_down, itok_B_2_6, 0), L0_ffn_weight, L0_ffn_bias)
    x = x + _L1_ffn_ref(_L1_cond_ref(x, L1_cond_A, L1_cond_B, itok_B_4_50), L1_ffn_lora_A, L1_ffn_lora_B, L1_ffn_W, L1_ffn_bias, L1_ffn_lora_weights)
    return x

_drawn_inputs = setup_inputs


def setup_inputs(seed=0):
    import zlib

    import numpy as np

    out = dict(_drawn_inputs(seed))
    spreads = {'L1_ffn_lora_weights': (0.125, 0.2)}
    factors = {'L0_ffn_bias': 48.034, 'L1_ffn_bias': 200.0}
    for name, (base, spread) in spreads.items():
        noise = np.random.default_rng([zlib.crc32(name.encode()), seed]).standard_normal(out[name].shape)
        drawn = base * np.exp(spread * noise) if base else spread * noise
        out[name] = jnp.asarray(drawn.astype(out[name].dtype))
    for name, factor in factors.items():
        out[name] = (out[name] * factor).astype(out[name].dtype)
    return out
```

```python
from contextlib import ExitStack

import numpy as np

import concourse.bass as bass
from concourse import mybir

BATCH, SEQ, H = 128, 32, 512
F = 1376
RANK = 16
R0, R1 = 16, 64
N_LORA = 8
P = 128
TOKENS = BATCH * SEQ
G = TOKENS // P
GB = P // SEQ
KC = H // P
CHUNKS = [(0, 512), (512, 512), (1024, 352)]
BLOCKS = [(f, min(P, F - f)) for f in range(0, F, P)]
NBLK = len(BLOCKS)
CHUNK_BLOCKS = [range(0, 4), range(4, 8), range(8, 11)]
NC = len(CHUNKS)
RING_LAG = [0, -1, 1]
ACT_SLOT = [0, 1, 0]
ACTT_SLOT = [0, 4, 0]
AW = KC * 2 * RANK
ADW = NBLK * RANK
GR = GB * RANK
MW = H + GR
MH = MW // 2
LORA0_SCALE = 0.5
LORA1_SCALE = 2.0
A1_RING = 3
W_RING = 5

f32 = mybir.dt.float32
f32r = mybir.dt.float32r
i32 = mybir.dt.int32
ALU = mybir.AluOpType
ACT = mybir.ActivationFunctionType


def constants():
    p = np.arange(P)
    ident = np.eye(P, dtype=np.float32)
    own = (p[:, None] // SEQ == np.arange(GR)[None, :] // RANK) * np.float32(LORA0_SCALE)
    own_tok = np.concatenate([own, own], axis=1).astype(np.float32)
    own_row = (p[:, None] // (2 * RANK) == p[None, :] // SEQ).astype(np.float32)
    idx = np.zeros((P, 11), np.float32)
    for b in range(GB):
        idx[:, b] = RANK * ((p % GR) // RANK == b)
        idx[:, 5 + b] = RANK * (p // (2 * RANK) == b)
    idx[:, 4] = idx[:, 9] = p % RANK
    idx[:, 10] = p
    return np.concatenate([ident, own_tok, own_row, idx], axis=1).astype(np.float32)


CONST_W = 3 * P + 11


def build_adaln_ffn(nc, xT, x, wgu, signT, wd, bd, btab, atab, la, lbT, lw, w1T, a1, b1tab,
                    bias0, bias1, id0, id1, consts, sb_table, c_table, out):
    ctx = ExitStack()
    with ctx:
        base = (nc.sbuf_base + 31) // 32 * 32
        cursor = [base]

        def place(name, shape, dtype, at=None):
            n = 4 * int(np.prod(shape[1:]))
            n = (n + 31) // 32 * 32
            if at is None:
                at = cursor
            t = nc.alloc_sbuf_tensor_at(name, shape, dtype, offset=at[0])
            at[0] += n
            return t

        w_at = [cursor[0]]
        w_sb = place("w_sb", [P, 2, 2, KC, F], f32r)
        down_sb = place("down_sb", [P, NBLK, 2, MW], f32r)
        loop_at = [cursor[0]]
        b_sb = [place(f"b_sb{c}", [P, 2 * w], f32r) for c, (_, w) in enumerate(CHUNKS)]
        b_raw = place("b_raw", [P, 1024], f32)
        a_raw = place("a_raw", [P, GB, AW + ADW], f32)
        a_sb = place("a_sb", [P, KC, GB, 2, 2 * RANK], f32r)
        xT_raw = place("xT_raw", [P, KC, P], f32)
        xT_sb = place("xT_sb", [P, KC, 2, P], f32r)
        x_sb = place("x_sb", [P, H], f32)
        x1T_sb = place("x1T_sb", [P, KC, 2, P], f32r)
        act_sb = place("act_sb", [P, 2, 512], f32)
        actT_sb = place("actT_sb", [P, 8, 2, P], f32r)
        t_sum = place("t_sum", [P, 2 * GR], f32)
        t_own = place("t_own", [P, 2, 2, GR], f32)
        tT_sb = place("tT_sb", [P, 2, 2, P], f32r)
        td_own = place("td_own", [P, 2, GR], f32)
        tdT_sb = place("tdT_sb", [P, 2, P], f32r)
        t1_sum = place("t1_sum", [P, P], f32)
        t1_sb = place("t1_sb", [P, 2, P], f32r)
        row_raw = place("row_raw", [P, H], f32)
        sbd_sb = place("sbd_sb", [P, H], f32r)
        c_sb = place("c_sb", [P, 2, H], f32r)
        b1_raw = place("b1_raw", [P, GB, KC * RANK], f32)
        b1_sb = place("b1_sb", [P, KC, GB, 2, RANK], f32r)
        loop_end = cursor[0]
        bias_sb = place("bias_sb", [P, 2, H], f32)
        const_sb = place("const_sb", [P, CONST_W], f32)
        idx_rows = place("idx_rows", [P, 2, G], i32)
        idx_feat = place("idx_feat", [P, 2, BATCH], i32)
        now = place("now", [P, 2 * GB + 4], i32)
        now_a, now_b1 = now[:, 0:GB], now[:, GB:2 * GB]
        now_b, now_sb, now_c, zero = (now[:, 2 * GB + n:2 * GB + n + 1] for n in range(4))
        assert cursor[0] <= nc.sbuf_usable_end, (cursor[0], nc.sbuf_usable_end)
        ident = const_sb[:, 0:P]
        own_tok = const_sb[:, P:2 * P]
        own_row = const_sb[:, 2 * P:3 * P]
        idx_c = const_sb[:, 3 * P:CONST_W]

        sign_sb = place("sign_sb", [P, KC, H], f32r, w_at)
        wd_sb = place("wd_sb", [P, 2, KC, F], f32r, w_at)
        weff_sb = place("weff_sb", [P, 2, KC, H], f32r, w_at)
        a1_sb = place("a1_sb", [P, A1_RING, 2, KC, P], f32r, w_at)
        rows_out = place("rows_out", [P, 3, H], f32, w_at)
        assert w_at[0] <= loop_at[0] - 4 * NBLK * 2 * MW
        wd_raw = place("wd_raw", [P, KC, F], f32, loop_at)
        a1_at = [loop_at[0] - 4 * KC * F]
        a1_raw = place("a1_raw", [P, 8, KC, P], f32, a1_at)
        sign_raw = place("sign_raw", [P, KC, H], f32, loop_at)
        wraw_at = [loop_at[0]]
        bd_raw = place("bd_raw", [P, KC, R0 * RANK], f32, loop_at)
        bd_sb = place("bd_sb", [P, 2, KC, R0 * RANK], f32r, loop_at)
        la_raw = place("la_raw", [P, H], f32, loop_at)
        la_sb = place("la_sb", [P, 2, H], f32r, loop_at)
        lb_raw = place("lb_raw", [P, H], f32, loop_at)
        lb_sb = place("lb_sb", [P, 2, H], f32r, loop_at)
        w1_raw = place("w1_raw", [P, KC, H], f32, loop_at)
        id_raw = place("id_raw", [P, 2, BATCH], i32, loop_at)
        id_f = place("id_f", [P, 2, BATCH], f32, loop_at)
        id_acc = place("id_acc", [P, 2, G], f32, loop_at)
        lw_sb = place("lw_sb", [P, 2], f32, loop_at)
        assert loop_at[0] <= loop_end, (loop_at[0], loop_end)
        w_raw = place("w_raw", [P, W_RING, F], f32, wraw_at)
        assert wraw_at[0] <= loop_end

        def bank(name):
            return ctx.enter_context(nc.psum_tensor(name, [P, 512], f32))

        gate_ps, up_ps = bank("gate_ps"), bank("up_ps")
        y_ps = [bank("y0_ps"), bank("y1_ps")]
        actT_ps, x1T_ps, sum_ps, tT_ps = bank("actT_ps"), bank("x1T_ps"), bank("sum_ps"), bank("tT_ps")
        ring_ps = [gate_ps, up_ps, y_ps[0], y_ps[1]]

        def sem(name):
            return ctx.enter_context(nc.semaphore(name))

        names = ("const_in", "bias_in", "id_in", "sign_in", "wd_in", "bd_in", "la_in", "lb_in", "w1_in", "a1_in",
                 "sign_done", "wd_hi", "wd_lo", "bd_hi", "bd_lo", "la_hi", "la_lo", "lb_scaled", "lb_hi", "lb_lo",
                 "ids_done", "dve_step", "down_mm", "down_hi", "down_lo", "sbd_mm", "sbd_out", "weff_mm", "weff_sum",
                 "weff_hi", "weff_lo", "a1_hi", "a1_lo", "c_mm", "c_out", "tab_stored", "w_hi", "w_lo")
        S = {n: sem("pro_" + n) for n in names}
        w_in = [sem(f"pro_w_in{k}") for k in range(W_RING)]
        rows_free = [sem(f"pro_rows_free{k}") for k in range(3)]
        names = ("xT_in", "xT_hi", "xT_lo", "x_in", "x_biased", "gate_mm", "up_mm", "silu_done", "act_done",
                 "act_tr", "actT_hi", "actT_lo", "down_mm", "a_in", "a_hi", "a_lo", "ad_hi", "ad_lo", "t_mm", "t_added",
                 "t_masked", "t_tr", "tT_hi", "tT_lo", "td_masked", "td_tr", "tdT_hi", "tdT_lo", "y_mm", "x1_done",
                 "x1_tr", "x1T_hi", "x1T_lo", "x1_biased", "b1_in", "b1_hi", "b1_lo", "t1_mm", "t1_added", "t1_masked",
                 "t1_hi", "t1_lo", "c_in", "c_hi", "c_lo", "out_mm", "out_done", "stored", "b_in", "b_hi", "b_lo",
                 "sbd_in", "sbd_hi", "sbd_lo", "idx_a", "idx_b", "idx_sb", "idx_b1", "idx_c")
        L = {n: sem(n) for n in names}
        block = ctx.enter_context(nc.Block())

        def after(engine, semaphore, count):
            if not isinstance(count, int) or count > 0:
                engine.wait_ge(semaphore, count)

        def hi(t):
            return t.bitcast(f32)

        N_W = 2 * KC

        @block.sync
        def _(sp):
            sp.dma_start(sign_raw[:], signT).then_inc(S["sign_in"], 16)
            sp.dma_start(wd_raw[:], wd).then_inc(S["wd_in"], 16)
            sp.dma_start(bd_raw[:], bd).then_inc(S["bd_in"], 16)
            sp.dma_start(la_raw[:], la).then_inc(S["la_in"], 16)
            sp.dma_start(lb_raw[:], lbT).then_inc(S["lb_in"], 16)
            sp.dma_start(lw_sb[:, 0:1], lw).then_inc(S["lb_in"], 16)
            sp.dma_start(w1_raw[:], w1T).then_inc(S["w1_in"], 16)
            sp.wait_ge(S["wd_lo"], KC)
            sp.dma_start(a1_raw[:], a1).then_inc(S["a1_in"], 16)
            for n in range(2):
                sp.wait_ge(S["sbd_out"], n + 1)
                sp.dma_start(sb_table[n * P:(n + 1) * P, :], rows_out[:, n, :]).then_inc(rows_free[n], 16)
            sp.wait_ge(S["weff_lo"], KC)
            for k in range(W_RING):
                sp.dma_start(w_raw[:, k, :], wgu[:, k, :]).then_inc(w_in[k], 16)
            for n in range(8):
                k = (2 + n) % 3
                sp.wait_ge(S["c_out"], n + 1)
                sp.dma_start(c_table[n * P:(n + 1) * P, :], rows_out[:, k, :]).then_inc(rows_free[k], 16)
            for k in range(W_RING, N_W):
                sp.wait_ge(S["w_lo"], k - W_RING + 1)
                sp.dma_start(w_raw[:, k % W_RING, :], wgu[:, k, :]).then_inc(w_in[k % W_RING], 16)

            def load_xT(g):
                after(sp, L["xT_lo"], g)
                sp.dma_start(xT_raw[:], xT[bass.ds(g * P, P), :].rearrange("p (k t) -> p k t", k=KC)
                             ).then_inc(L["xT_in"], 16)

            def load_x(g):
                after(sp, L["stored"], 16 * g)
                sp.dma_start(x_sb[:], x[bass.ds(g * P, P), :]).then_inc(L["x_in"], 16)

            def store(g):
                sp.wait_ge(L["out_done"], g + 1)
                sp.dma_start(out[bass.ds(g * P, P), :], x_sb[:]).then_inc(L["stored"], 16)

            sp.wait_ge(S["w_lo"], N_W)
            load_xT(0)
            load_x(0)
            load_xT(1)
            with sp.Fori(1, G - 1) as g:
                load_xT(g + 1)
                store(g - 1)
                load_x(g)
            store(G - 2)
            load_x(G - 1)
            store(G - 1)
            sp.wait_ge(L["stored"], 16 * G)

        @block.gpsimd
        def _(pool):
            pool.dma_start(const_sb[:], consts).then_inc(S["const_in"], 16)
            pool.dma_start(id_raw[:, 0, :], id0.to_broadcast([P, BATCH])).then_inc(S["id_in"], 16)
            pool.dma_start(id_raw[:, 1, :], id1.to_broadcast([P, BATCH])).then_inc(S["id_in"], 16)
            pool.dma_start(bias_sb[:, 0, :], bias0.to_broadcast([P, H])).then_inc(S["bias_in"], 16)
            pool.dma_start(bias_sb[:, 1, :], bias1.to_broadcast([P, H])).then_inc(S["bias_in"], 16)
            nc.gpsimd.memset(zero, 0).then_inc(S["ids_done"], 1)
            pool.wait_ge(S["ids_done"], 5)
            pool.wait_ge(S["bias_in"], 32)
            pool.wait_ge(S["w_lo"], N_W)
            for k in range(3):
                pool.wait_ge(rows_free[k], 16 * len([n for n in range(10) if n % 3 == k]))

            def gather(dst, index, table, signal):
                nc.gpsimd.indirect_dma_start(
                    out=dst, out_offset=None, in_=table,
                    in_offset=bass.IndirectOffsetOnAxis(ap=index, axis=0)).then_inc(signal, 16)

            def gather_a(g):
                after(pool, L["ad_lo"], g)
                nc.gpsimd.tensor_copy(now_a, idx_feat[:, 0, bass.ds(g * GB, GB)]).then_inc(L["idx_a"], 1)
                pool.wait_ge(L["idx_a"], 1)
                pool.sem_clear(L["idx_a"])
                for b in range(GB):
                    gather(a_raw[:, b, :], now_a[:, b:b + 1], atab, L["a_in"])

            def gather_b(g, c):
                after(pool, L["b_lo"], g * NC + c)
                if c == 0:
                    last = nc.gpsimd.tensor_copy(now_b, idx_rows[:, 0, bass.ds(g, 1)])
                else:
                    last = nc.gpsimd.tensor_tensor(now_b, now_b, zero, ALU.add)
                last.then_inc(L["idx_b"], 1)
                pool.wait_ge(L["idx_b"], 1)
                pool.sem_clear(L["idx_b"])
                gather(b_raw[:, 0:2 * CHUNKS[c][1]], now_b, btab[c], L["b_in"])

            def gather_sbd(g):
                after(pool, L["c_lo"], g)
                nc.gpsimd.tensor_copy(now_sb, idx_rows[:, 0, bass.ds(g, 1)]).then_inc(L["idx_sb"], 1)
                pool.wait_ge(L["idx_sb"], 1)
                pool.sem_clear(L["idx_sb"])
                gather(row_raw[:], now_sb, sb_table, L["sbd_in"])

            def gather_b1(g):
                after(pool, L["b1_lo"], g)
                nc.gpsimd.tensor_copy(now_b1, idx_feat[:, 1, bass.ds(g * GB, GB)]).then_inc(L["idx_b1"], 1)
                pool.wait_ge(L["idx_b1"], 1)
                pool.sem_clear(L["idx_b1"])
                for b in range(GB):
                    gather(b1_raw[:, b, :], now_b1[:, b:b + 1], b1tab, L["b1_in"])

            def gather_c(g):
                pool.wait_ge(L["sbd_lo"], g + 1)
                nc.gpsimd.tensor_copy(now_c, idx_rows[:, 1, bass.ds(g, 1)]).then_inc(L["idx_c"], 1)
                pool.wait_ge(L["idx_c"], 1)
                pool.sem_clear(L["idx_c"])
                gather(row_raw[:], now_c, c_table, L["c_in"])

            def add_bias0(g):
                pool.wait_ge(L["x_in"], 16 * g + 16)
                nc.gpsimd.tensor_tensor(x_sb[:], x_sb[:], bias_sb[:, 0, :], ALU.add).then_inc(L["x_biased"], 1)

            def add_bias1(g):
                pool.wait_ge(L["x1_tr"], g + 1)
                nc.gpsimd.tensor_tensor(x_sb[:], x_sb[:], bias_sb[:, 1, :], ALU.add).then_inc(L["x1_biased"], 1)

            def step(g, prev, nxt):
                if prev is not None:
                    add_bias0(prev)
                if nxt is not None:
                    gather_b(nxt, 0)
                    gather_a(nxt)
                if g is not None:
                    gather_sbd(g)
                    gather_b1(g)
                if prev is not None:
                    add_bias1(prev)
                if nxt is not None:
                    gather_b(nxt, 1)
                if g is not None:
                    gather_c(g)
                if nxt is not None:
                    gather_b(nxt, 2)

            gather_a(0)
            for c in range(NC):
                gather_b(0, c)
            step(0, None, 1)
            with pool.Fori(1, G - 1) as g:
                step(g, g - 1, g + 1)
            step(G - 1, G - 2, None)
            step(None, G - 1, None)

        @block.scalar
        def _(act):
            def copy(o, i):
                return nc.scalar.copy(o, i)

            act.wait_ge(S["sign_in"], 16)
            nc.scalar.activation(sign_sb[:], sign_raw[:], ACT.Sign).then_inc(S["sign_done"], 1)
            act.wait_ge(S["wd_in"], 16)
            for k in range(KC):
                copy(wd_sb[:, 0, k, :], wd_raw[:, k, :]).then_inc(S["wd_hi"], 1)
            act.wait_ge(S["bd_in"], 16)
            copy(bd_sb[:, 0, :, :], bd_raw[:]).then_inc(S["bd_hi"], 1)
            act.wait_ge(S["la_in"], 16)
            copy(la_sb[:, 0, :], la_raw[:]).then_inc(S["la_hi"], 1)
            act.wait_ge(S["lb_scaled"], 1)
            copy(lb_sb[:, 0, :], lb_raw[:]).then_inc(S["lb_hi"], 1)
            for n, (_, m) in enumerate(BLOCKS):
                act.wait_ge(S["down_mm"], n + 1)
                copy(down_sb[0:m, n, 0, 0:H], ring_ps[n % 4][0:m, :]).then_inc(S["down_hi"], 1)
            for n in range(2):
                act.wait_ge(S["sbd_mm"], n + 1)
                copy(rows_out[:, n, :], ring_ps[(NBLK + n) % 4][:]).then_inc(S["sbd_out"], 1)
            for k in range(KC):
                act.wait_ge(S["weff_sum"], k + 1)
                copy(weff_sb[:, 0, k, :], w1_raw[:, k, :]).then_inc(S["weff_hi"], 1)
            act.wait_ge(S["a1_in"], 16)

            def split_a1(n):
                after(act, S["c_mm"], n - A1_RING + 1)
                copy(a1_sb[:, n % A1_RING, 0, :, :], a1_raw[:, n, :, :]).then_inc(S["a1_hi"], 1)

            for n in range(A1_RING):
                split_a1(n)
            for n in range(8):
                k = (2 + n) % 3
                act.wait_ge(S["c_mm"], n + 1)
                after(act, rows_free[k], 16 * ((2 + n) // 3))
                copy(rows_out[:, k, :], ring_ps[(NBLK + 2 + KC + n) % 4][:]).then_inc(S["c_out"], 1)
                if n + A1_RING < 8:
                    split_a1(n + A1_RING)
            for k in range(3):
                act.wait_ge(rows_free[k], 16 * len([n for n in range(10) if n % 3 == k]))
            for n in range(N_W):
                act.wait_ge(w_in[n % W_RING], 16 * (n // W_RING + 1))
                copy(w_sb[:, n // KC, 0, n % KC, :], w_raw[:, n % W_RING, :]).then_inc(S["w_hi"], 1)
            act.wait_ge(S["w_lo"], N_W)

            def split_xT(g):
                act.wait_ge(L["xT_in"], 16 * g + 16)
                after(act, L["up_mm"], g * NC)
                copy(xT_sb[:, :, 0, :], xT_raw[:]).then_inc(L["xT_hi"], 1)

            def split_a(g):
                act.wait_ge(L["a_in"], 16 * GB * g + 16 * GB)
                after(act, L["t_mm"], g)
                for b in range(GB):
                    last = copy(a_sb[:, :, b, 0, :], a_raw[:, b, 0:AW].rearrange("p (k r) -> p k r", k=KC))
                last.then_inc(L["a_hi"], 1)

            def split_ad(g):
                act.wait_ge(L["a_in"], 16 * GB * g + 16 * GB)
                after(act, L["down_mm"], g * NC)
                for b in range(GB):
                    last = copy(down_sb[:, :, 0, H + b * RANK:H + (b + 1) * RANK],
                                a_raw[:, b, AW:].rearrange("p (n r) -> p n r", n=NBLK))
                last.then_inc(L["ad_hi"], 1)

            def split_b(g, c):
                act.wait_ge(L["b_in"], 16 * (g * NC + c) + 16)
                after(act, L["up_mm"], (g - 1) * NC + c + 1)
                copy(b_sb[c][:], b_raw[:, 0:2 * CHUNKS[c][1]]).then_inc(L["b_hi"], 1)

            def split_sbd(g):
                act.wait_ge(L["sbd_in"], 16 * g + 16)
                after(act, L["y_mm"], g)
                copy(sbd_sb[:], row_raw[:]).then_inc(L["sbd_hi"], 1)

            def split_b1(g):
                act.wait_ge(L["b1_in"], 16 * GB * g + 16 * GB)
                after(act, L["t1_mm"], g)
                for b in range(GB):
                    last = copy(b1_sb[:, :, b, 0, :], b1_raw[:, b, :].rearrange("p (k r) -> p k r", k=KC))
                last.then_inc(L["b1_hi"], 1)

            def split_c(g):
                act.wait_ge(L["c_in"], 16 * g + 16)
                after(act, L["out_mm"], g)
                copy(c_sb[:, 0, :], row_raw[:]).then_inc(L["c_hi"], 1)

            def silu(g, c):
                w = CHUNKS[c][1]
                act.wait_ge(L["gate_mm"], g * NC + c + 1)
                after(act, L["act_tr"], g * NC + RING_LAG[c])
                nc.scalar.activation(act_sb[:, ACT_SLOT[c], 0:w], gate_ps[:, 0:w], ACT.Silu).then_inc(L["silu_done"], 1)

            def split_actT(g, c):
                n = len(CHUNK_BLOCKS[c])
                act.wait_ge(L["act_tr"], g * NC + c + 1)
                after(act, L["down_mm"], g * NC + RING_LAG[c])
                copy(actT_sb[:, ACTT_SLOT[c]:ACTT_SLOT[c] + n, 0, :],
                     actT_ps[:, 0:n * P].rearrange("p (n t) -> p n t", n=n)).then_inc(L["actT_hi"], 1)

            def split_t(g):
                act.wait_ge(L["t_tr"], g + 1)
                after(act, L["up_mm"], g * NC)
                copy(tT_sb[:, 0, :, :], tT_ps[:, 0:2 * P].rearrange("p (u t) -> p u t", u=2)).then_inc(L["tT_hi"], 1)

            def split_td(g):
                act.wait_ge(L["td_tr"], g + 1)
                after(act, L["y_mm"], g)
                copy(tdT_sb[:, 0, :], tT_ps[:, 0:P]).then_inc(L["tdT_hi"], 1)

            def split_x1(g):
                act.wait_ge(L["x1_tr"], g + 1)
                after(act, L["t1_mm"], g)
                copy(x1T_sb[:, :, 0, :], x1T_ps[:].rearrange("p (k t) -> p k t", k=KC)).then_inc(L["x1T_hi"], 1)

            def split_t1(g):
                act.wait_ge(L["t1_masked"], g + 1)
                after(act, L["out_mm"], g)
                copy(t1_sb[:, 0, :], t1_sum[:]).then_inc(L["t1_hi"], 1)

            def step(g, prev, nxt):
                if g is not None:
                    split_ad(g)
                    silu(g, 0)
                if prev is not None:
                    split_td(prev)
                if g is not None:
                    split_sbd(g)
                    silu(g, 1)
                    split_actT(g, 0)
                if prev is not None:
                    split_x1(prev)
                if nxt is not None:
                    split_b(nxt, 0)
                if prev is not None:
                    split_t1(prev)
                if g is not None:
                    split_b1(g)
                    silu(g, 2)
                    split_actT(g, 1)
                if nxt is not None:
                    split_a(nxt)
                    split_xT(nxt)
                    split_b(nxt, 1)
                if g is not None:
                    split_actT(g, 2)
                if nxt is not None:
                    split_t(nxt)
                if g is not None:
                    split_c(g)
                if nxt is not None:
                    split_b(nxt, 2)

            split_xT(0)
            split_a(0)
            split_t(0)
            for c in range(NC):
                split_b(0, c)
            step(0, None, 1)
            with act.Fori(1, G - 1) as g:
                step(g, g - 1, g + 1)
            step(G - 1, G - 2, None)
            step(None, G - 1, None)

        @block.vector
        def _(dve):
            def lo(o, whole, high):
                return nc.vector.tensor_tensor(o, whole, hi(high), ALU.subtract)

            steps = [0]

            def link(instruction):
                steps[0] += 1
                instruction.then_inc(S["dve_step"], 1)
                dve.wait_ge(S["dve_step"], steps[0])

            dve.wait_ge(S["id_in"], 32)
            dve.wait_ge(S["const_in"], 16)
            for n, count in enumerate((R0, R1)):
                link(nc.vector.tensor_scalar(id_f[:, n, :], id_raw[:, n, :], float(count - 1), 0.0, ALU.min, ALU.max))
                nc.vector.tensor_scalar(idx_feat[:, n, :], id_f[:, n, :], float(P), idx_c[:, 10:11],
                                        ALU.mult, ALU.add).then_inc(S["ids_done"], 1)
                own = id_f[:, n, :].rearrange("p (g b) -> p b g", b=GB)
                link(nc.vector.tensor_scalar(id_acc[:, n, :], own[:, 0, :], idx_c[:, 5 * n:5 * n + 1],
                                             idx_c[:, 5 * n + 4:5 * n + 5], ALU.mult, ALU.add))
                for b in range(1, GB):
                    to = idx_rows if b == GB - 1 else id_acc
                    last = nc.vector.scalar_tensor_tensor(to[:, n, :], own[:, b, :], idx_c[:, 5 * n + b:5 * n + b + 1],
                                                          id_acc[:, n, :], ALU.mult, ALU.add)
                    if b < GB - 1:
                        link(last)
                last.then_inc(S["ids_done"], 1)
            for k in range(KC):
                dve.wait_ge(S["wd_hi"], k + 1)
                lo(wd_sb[:, 1, k, :], wd_raw[:, k, :], wd_sb[:, 0, k, :]).then_inc(S["wd_lo"], 1)
            dve.wait_ge(S["bd_hi"], 1)
            lo(bd_sb[:, 1, :, :], bd_raw[:], bd_sb[:, 0, :, :]).then_inc(S["bd_lo"], 1)
            dve.wait_ge(S["la_hi"], 1)
            lo(la_sb[:, 1, :], la_raw[:], la_sb[:, 0, :]).then_inc(S["la_lo"], 1)
            dve.wait_ge(S["lb_in"], 32)
            link(nc.vector.tensor_scalar(lw_sb[:, 1:2], lw_sb[:, 0:1], LORA1_SCALE, None, ALU.mult))
            nc.vector.tensor_scalar(lb_raw[:], lb_raw[:], lw_sb[:, 1:2], None, ALU.mult).then_inc(S["lb_scaled"], 1)
            dve.wait_ge(S["lb_hi"], 1)
            lo(lb_sb[:, 1, :], lb_raw[:], lb_sb[:, 0, :]).then_inc(S["lb_lo"], 1)
            for n, (_, m) in enumerate(BLOCKS):
                dve.wait_ge(S["down_hi"], n + 1)
                lo(down_sb[0:m, n, 1, 0:H], ring_ps[n % 4][0:m, :], down_sb[0:m, n, 0, 0:H]).then_inc(S["down_lo"], 1)
            dve.wait_ge(S["w1_in"], 16)
            for k in range(KC):
                dve.wait_ge(S["weff_mm"], k + 1)
                nc.vector.tensor_tensor(w1_raw[:, k, :], w1_raw[:, k, :], ring_ps[(NBLK + 2 + k) % 4][:],
                                        ALU.add).then_inc(S["weff_sum"], 1)
            for k in range(KC):
                dve.wait_ge(S["weff_hi"], k + 1)
                lo(weff_sb[:, 1, k, :], w1_raw[:, k, :], weff_sb[:, 0, k, :]).then_inc(S["weff_lo"], 1)
            for n in range(8):
                dve.wait_ge(S["a1_hi"], n + 1)
                lo(a1_sb[:, n % A1_RING, 1, :, :], a1_raw[:, n, :, :], a1_sb[:, n % A1_RING, 0, :, :]
                   ).then_inc(S["a1_lo"], 1)
            for n in range(N_W):
                dve.wait_ge(S["w_hi"], n + 1)
                lo(w_sb[:, n // KC, 1, n % KC, :], w_raw[:, n % W_RING, :], w_sb[:, n // KC, 0, n % KC, :]
                   ).then_inc(S["w_lo"], 1)

            def split_xT(g):
                dve.wait_ge(L["xT_hi"], g + 1)
                lo(xT_sb[:, :, 1, :], xT_raw[:], xT_sb[:, :, 0, :]).then_inc(L["xT_lo"], 1)

            def split_a(g):
                dve.wait_ge(L["a_hi"], g + 1)
                for b in range(GB):
                    last = lo(a_sb[:, :, b, 1, :], a_raw[:, b, 0:AW].rearrange("p (k r) -> p k r", k=KC),
                              a_sb[:, :, b, 0, :])
                last.then_inc(L["a_lo"], 1)

            def split_ad(g):
                dve.wait_ge(L["ad_hi"], g + 1)
                for b in range(GB):
                    cols = slice(H + b * RANK, H + (b + 1) * RANK)
                    last = lo(down_sb[:, :, 1, cols], a_raw[:, b, AW:].rearrange("p (n r) -> p n r", n=NBLK),
                              down_sb[:, :, 0, cols])
                last.then_inc(L["ad_lo"], 1)

            def split_b(g, c):
                dve.wait_ge(L["b_hi"], g * NC + c + 1)
                lo(b_sb[c][GR:, :], b_raw[GR:, 0:2 * CHUNKS[c][1]], b_sb[c][GR:, :]).then_inc(L["b_lo"], 1)

            def split_sbd(g):
                dve.wait_ge(L["sbd_hi"], g + 1)
                lo(sbd_sb[GR:, :], row_raw[GR:, :], sbd_sb[GR:, :]).then_inc(L["sbd_lo"], 1)

            def split_b1(g):
                dve.wait_ge(L["b1_hi"], g + 1)
                for b in range(GB):
                    last = lo(b1_sb[:, :, b, 1, :], b1_raw[:, b, :].rearrange("p (k r) -> p k r", k=KC),
                              b1_sb[:, :, b, 0, :])
                last.then_inc(L["b1_lo"], 1)

            def split_c(g):
                dve.wait_ge(L["c_hi"], g + 1)
                lo(c_sb[:, 1, :], row_raw[:], c_sb[:, 0, :]).then_inc(L["c_lo"], 1)

            def gated(g, c):
                w = CHUNKS[c][1]
                dve.wait_ge(L["up_mm"], g * NC + c + 1)
                dve.wait_ge(L["silu_done"], g * NC + c + 1)
                a = act_sb[:, ACT_SLOT[c], 0:w]
                nc.vector.tensor_tensor(a, a, up_ps[:, 0:w], ALU.mult).then_inc(L["act_done"], 1)

            def split_actT(g, c):
                n, at = len(CHUNK_BLOCKS[c]), ACTT_SLOT[c]
                dve.wait_ge(L["actT_hi"], g * NC + c + 1)
                lo(actT_sb[:, at:at + n, 1, :], actT_ps[:, 0:n * P].rearrange("p (n t) -> p n t", n=n),
                   actT_sb[:, at:at + n, 0, :]).then_inc(L["actT_lo"], 1)

            def own_t(g):
                dve.wait_ge(L["t_mm"], g + 1)
                s = sum_ps[:, 0:4 * GR].rearrange("p (b h u r) -> p h u b r", b=GB, h=2, u=2)
                t = t_sum[:].rearrange("p (u b r) -> p u b r", u=2, b=GB)
                nc.vector.tensor_copy(t, s[:, 0]).then_inc(L["t_added"], 1)
                dve.wait_ge(L["t_added"], 2 * g + 1)
                nc.vector.tensor_tensor(t, t, s[:, 1], ALU.add).then_inc(L["t_added"], 1)
                dve.wait_ge(L["t_added"], 2 * g + 2)
                after(dve, L["t_tr"], g)
                for d in range(2):
                    last = nc.vector.tensor_tensor(t_own[:, :, d, :], t_sum[:].rearrange("p (u r) -> p u r", u=2),
                                                   own_tok.rearrange("p (u r) -> p u r", u=2), ALU.mult)
                last.then_inc(L["t_masked"], 1)

            def split_t(g):
                dve.wait_ge(L["tT_hi"], g + 1)
                lo(tT_sb[:, 1, :, :], tT_ps[:, 0:2 * P].rearrange("p (u t) -> p u t", u=2), tT_sb[:, 0, :, :]
                   ).then_inc(L["tT_lo"], 1)

            def own_td(g):
                dve.wait_ge(L["down_mm"], g * NC + NC)
                after(dve, L["td_tr"], g)
                for d in range(2):
                    last = nc.vector.tensor_tensor(td_own[:, d, :], y_ps[1][:, H - MH:MH], own_tok[:, 0:GR], ALU.mult)
                last.then_inc(L["td_masked"], 1)

            def split_td(g):
                dve.wait_ge(L["tdT_hi"], g + 1)
                lo(tdT_sb[:, 1, :], tT_ps[:, 0:P], tdT_sb[:, 0, :]).then_inc(L["tdT_lo"], 1)

            def add_y(g):
                dve.wait_ge(L["y_mm"], g + 1)
                dve.wait_ge(L["x_biased"], g + 1)
                nc.vector.tensor_tensor(x_sb[:, 0:MH], x_sb[:, 0:MH], y_ps[0][:, 0:MH], ALU.add)
                nc.vector.tensor_tensor(x_sb[:, MH:H], x_sb[:, MH:H], y_ps[1][:, 0:H - MH],
                                        ALU.add).then_inc(L["x1_done"], 1)

            def split_x1(g):
                dve.wait_ge(L["x1T_hi"], g + 1)
                lo(x1T_sb[:, :, 1, :], x1T_ps[:].rearrange("p (k t) -> p k t", k=KC), x1T_sb[:, :, 0, :]
                   ).then_inc(L["x1T_lo"], 1)

            def own_t1(g):
                dve.wait_ge(L["t1_mm"], g + 1)
                nc.vector.tensor_copy(t1_sum[:], sum_ps[:, 0:P]).then_inc(L["t1_added"], 1)
                dve.wait_ge(L["t1_added"], 2 * g + 1)
                nc.vector.tensor_tensor(t1_sum[:], t1_sum[:], sum_ps[:, P:2 * P], ALU.add).then_inc(L["t1_added"], 1)
                dve.wait_ge(L["t1_added"], 2 * g + 2)
                nc.vector.tensor_tensor(t1_sum[:], t1_sum[:], own_row, ALU.mult).then_inc(L["t1_masked"], 1)
                dve.wait_ge(L["t1_hi"], g + 1)
                lo(t1_sb[:, 1, :], t1_sum[:], t1_sb[:, 0, :]).then_inc(L["t1_lo"], 1)

            def add_out(g):
                dve.wait_ge(L["out_mm"], g + 1)
                dve.wait_ge(L["x1_biased"], g + 1)
                nc.vector.tensor_tensor(x_sb[:], x_sb[:], sum_ps[:], ALU.add).then_inc(L["out_done"], 1)

            def step(g, prev, nxt):
                if prev is not None:
                    own_td(prev)
                if g is not None:
                    split_ad(g)
                if prev is not None:
                    split_td(prev)
                if g is not None:
                    gated(g, 0)
                if prev is not None:
                    add_y(prev)
                if g is not None:
                    split_sbd(g)
                    split_actT(g, 0)
                if prev is not None:
                    split_x1(prev)
                if g is not None:
                    gated(g, 1)
                if nxt is not None:
                    split_b(nxt, 0)
                if prev is not None:
                    own_t1(prev)
                if g is not None:
                    split_b1(g)
                    split_actT(g, 1)
                if nxt is not None:
                    split_a(nxt)
                if g is not None:
                    gated(g, 2)
                if nxt is not None:
                    split_xT(nxt)
                if prev is not None:
                    add_out(prev)
                if nxt is not None:
                    split_b(nxt, 1)
                if g is not None:
                    split_actT(g, 2)
                if nxt is not None:
                    own_t(nxt)
                    split_t(nxt)
                if g is not None:
                    split_c(g)
                if nxt is not None:
                    split_b(nxt, 2)

            split_xT(0)
            split_a(0)
            own_t(0)
            split_t(0)
            for c in range(NC):
                split_b(0, c)
            step(0, None, 1)
            with dve.Fori(1, G - 1) as g:
                step(g, g - 1, g + 1)
            step(G - 1, G - 2, None)
            step(None, G - 1, None)

        @block.tensor
        def _(pe):
            def product(o, terms, signal, start=True, check=True):
                for n, (w, m) in enumerate(terms):
                    last = nc.tensor.matmul(o, w, m, start=start and n == 0, stop=n == len(terms) - 1,
                                            skip_group_check=not check)
                return last.then_inc(signal, 1) if signal is not None else last

            THREE = ((0, 0), (0, 1), (1, 0))

            pe.wait_ge(S["sign_done"], 1)
            pe.wait_ge(S["wd_lo"], KC)
            for n, (f, m) in enumerate(BLOCKS):
                after(pe, S["down_lo"], n - 3)
                product(ring_ps[n % 4][0:m, :], [(wd_sb[:, h, k, f:f + m], sign_sb[:, k, :])
                                                 for k in range(KC) for h in range(2)], S["down_mm"])
            pe.wait_ge(S["bd_lo"], 1)
            for n in range(2):
                pe.wait_ge(S["down_lo"], NBLK + n - 3)
                product(ring_ps[(NBLK + n) % 4][:], [(bd_sb[:, h, k, n * P:(n + 1) * P], sign_sb[:, k, :])
                                                     for k in range(KC) for h in range(2)], S["sbd_mm"])
            pe.wait_ge(S["la_lo"], 1)
            pe.wait_ge(S["lb_lo"], 1)
            for k in range(KC):
                n = NBLK + 2 + k
                if n - 4 < NBLK:
                    pe.wait_ge(S["down_lo"], n - 3)
                else:
                    pe.wait_ge(S["sbd_out"], n - 3 - NBLK)
                product(ring_ps[n % 4][:], [(la_sb[:, a, k * P:(k + 1) * P], lb_sb[:, b, :]) for a, b in THREE],
                        S["weff_mm"])
            pe.wait_ge(S["weff_lo"], KC)
            for n in range(8):
                at = NBLK + 2 + KC + n
                pe.wait_ge(S["a1_lo"], n + 1)
                after(pe, S["c_out"], n - 3)
                product(ring_ps[at % 4][:], [(a1_sb[:, n % A1_RING, a, k, :], weff_sb[:, b, k, :])
                                             for k in range(KC) for a, b in THREE], S["c_mm"])
            pe.wait_ge(S["c_out"], 8)
            pe.wait_ge(S["w_lo"], N_W)

            def t_product(g):
                pe.wait_ge(L["xT_lo"], g + 1)
                pe.wait_ge(L["a_lo"], g + 1)
                after(pe, L["t_masked"], g)
                after(pe, L["t1_masked"], g - 1)
                after(pe, L["out_done"], g - 1)
                product(sum_ps[:, 0:4 * GR], [(xT_sb[:, k, h, :], a_sb[:, k, :, :, :].rearrange("p b h r -> p (b h r)"))
                                              for k in range(KC) for h in range(2)], L["t_mm"])

            def t_transpose(g):
                pe.wait_ge(L["t_masked"], g + 1)
                after(pe, L["tdT_lo"], g - 1)
                for u in range(2):
                    last = nc.tensor.transpose(tT_ps[:, u * P:(u + 1) * P], t_own[:, u, :, :].rearrange("p d r -> p (d r)"), ident)
                last.then_inc(L["t_tr"], 1)

            def gate_up(g, c, u):
                f, w = CHUNKS[c]
                o = (gate_ps, up_ps)[u][:, 0:w]
                if c == 0 and u == 0:
                    pe.wait_ge(L["xT_lo"], g + 1)
                after(pe, L[("silu_done", "act_done")[u]], g * NC + c)
                for n, (k, a, b) in enumerate((k, a, b) for k in range(KC) for a, b in THREE):
                    nc.tensor.matmul(o, xT_sb[:, k, a, :], w_sb[:, u, b, k, f:f + w], start=n == 0, stop=False)
                if c == 0 and u == 0:
                    pe.wait_ge(L["tT_lo"], g + 1)
                if u == 0:
                    pe.wait_ge(L["b_lo"], g * NC + c + 1)
                for a in range(2):
                    last = nc.tensor.matmul(o, tT_sb[:, a, u, :], b_sb[c][:, u * w:(u + 1) * w], start=False,
                                            stop=a == 1)
                last.then_inc(L[("gate_mm", "up_mm")[u]], 1)

            def act_transpose(g, c):
                f, w = CHUNKS[c]
                pe.wait_ge(L["act_done"], g * NC + c + 1)
                after(pe, L["actT_lo"], g * NC + c)
                for n, blk in enumerate(CHUNK_BLOCKS[c]):
                    m = BLOCKS[blk][1]
                    last = nc.tensor.transpose(actT_ps[0:m, n * P:(n + 1) * P],
                                               act_sb[:, ACT_SLOT[c], n * P:n * P + m], ident)
                last.then_inc(L["act_tr"], 1)

            def down(g, c):
                pe.wait_ge(L["actT_lo"], g * NC + c + 1)
                if c == 0:
                    pe.wait_ge(L["ad_lo"], g + 1)
                    after(pe, L["x1_done"], g)
                for n, blk in enumerate(CHUNK_BLOCKS[c]):
                    m = BLOCKS[blk][1]
                    for a, b in THREE:
                        for half in range(2):
                            last = nc.tensor.matmul(
                                y_ps[half][:, 0:MH], actT_sb[0:m, ACTT_SLOT[c] + n, a, :],
                                down_sb[0:m, blk, b, half * MH:(half + 1) * MH],
                                start=blk == 0 and (a, b) == (0, 0), stop=blk == NBLK - 1 and (a, b) == (1, 0))
                last.then_inc(L["down_mm"], 1)

            def td_transpose(g):
                pe.wait_ge(L["td_masked"], g + 1)
                if isinstance(g, int) and g == G - 1:
                    pe.wait_ge(L["tT_lo"], G)
                else:
                    pe.wait_ge(L["tT_lo"], g + 2)
                nc.tensor.transpose(tT_ps[:, 0:P], td_own[:].rearrange("p d r -> p (d r)"), ident
                                    ).then_inc(L["td_tr"], 1)

            def down_lora(g):
                pe.wait_ge(L["tdT_lo"], g + 1)
                pe.wait_ge(L["sbd_lo"], g + 1)
                for a in range(2):
                    for half, (c0, c1) in enumerate(((0, MH), (MH, H))):
                        last = nc.tensor.matmul(y_ps[half][:, 0:c1 - c0], tdT_sb[:, a, :], sbd_sb[:, c0:c1],
                                                start=False, stop=a == 1, skip_group_check=True)
                last.then_inc(L["y_mm"], 1)

            def x1_transpose(g):
                pe.wait_ge(L["x1_done"], g + 1)
                after(pe, L["x1T_lo"], g)
                for k in range(KC):
                    last = nc.tensor.transpose(x1T_ps[:, k * P:(k + 1) * P], x_sb[:, k * P:(k + 1) * P], ident)
                last.then_inc(L["x1_tr"], 1)

            def t1_product(g):
                pe.wait_ge(L["x1T_lo"], g + 1)
                pe.wait_ge(L["b1_lo"], g + 1)
                if isinstance(g, int) and g == G - 1:
                    pe.wait_ge(L["t_masked"], G)
                else:
                    pe.wait_ge(L["t_masked"], g + 2)
                after(pe, L["out_done"], g)
                product(sum_ps[:, 0:2 * P], [(b1_sb[:, k, :, :, :].rearrange("p b h r -> p (b h r)"),
                                              x1T_sb[:, k, :, :].rearrange("p h t -> p (h t)"))
                                             for k in range(KC)], L["t1_mm"])

            def out_product(g):
                pe.wait_ge(L["t1_lo"], g + 1)
                pe.wait_ge(L["c_lo"], g + 1)
                product(sum_ps[:], [(t1_sb[:, a, :], c_sb[:, b, :]) for a, b in THREE], L["out_mm"])

            def step(g, prev, nxt):
                if g is not None:
                    gate_up(g, 0, 0)
                if prev is not None:
                    td_transpose(prev)
                if g is not None:
                    gate_up(g, 0, 1)
                if prev is not None:
                    down_lora(prev)
                if g is not None:
                    gate_up(g, 1, 0)
                    act_transpose(g, 0)
                if prev is not None:
                    x1_transpose(prev)
                if g is not None:
                    gate_up(g, 1, 1)
                if prev is not None:
                    t1_product(prev)
                if g is not None:
                    gate_up(g, 2, 0)
                    act_transpose(g, 1)
                    gate_up(g, 2, 1)
                if prev is not None:
                    out_product(prev)
                if g is not None:
                    down(g, 0)
                if nxt is not None:
                    t_product(nxt)
                if g is not None:
                    act_transpose(g, 2)
                    down(g, 1)
                if nxt is not None:
                    t_transpose(nxt)
                if g is not None:
                    down(g, 2)

            t_product(0)
            t_transpose(0)
            step(0, None, 1)
            with pe.Fori(1, G - 1) as g:
                step(g, g - 1, g + 1)
            step(G - 1, G - 2, None)
            step(None, G - 1, None)


def kernel(**inputs):
    import concourse.bacc as bacc
    from concourse.bass_utils import run_bass_kernel_spmd

    v = {n: np.ascontiguousarray(a) for n, a in inputs.items()}
    x = v["x"].reshape(TOKENS, H)
    feat = lambda a: a.reshape(KC, P, -1).transpose(1, 0, 2)
    gate_b = v["L0_cond_B_gate"][0].transpose(0, 2, 1).reshape(R0 * RANK, F)
    up_b = v["L0_cond_B_up"][0].transpose(0, 2, 1).reshape(R0 * RANK, F)
    a_rows = np.concatenate([v["L0_cond_A_gate"][0][:, None], v["L0_cond_A_up"][0][:, None]], axis=1)
    a_rows = a_rows.reshape(R0, 2, RANK, KC, P).transpose(0, 4, 3, 1, 2).reshape(R0 * P, AW)
    ad_rows = np.zeros((R0, RANK, NBLK * P), np.float32)
    ad_rows[:, :, 0:F] = v["L0_cond_A_down"][0]
    ad_rows = ad_rows.reshape(R0, RANK, NBLK, P).transpose(0, 3, 2, 1).reshape(R0 * P, ADW)
    arrays = {
        "xT": x.reshape(G, P, KC, P).transpose(0, 3, 2, 1).reshape(G * P, H),
        "x": x,
        "wgu": np.stack([feat(v["L0_cond_W_gate"].T), feat(v["L0_cond_W_up"].T)], axis=1).reshape(P, 2 * KC, F),
        "signT": feat(v["L0_ffn_weight"].T),
        "wd": feat(v["L0_cond_W_down"]),
        "bd": feat(v["L0_cond_B_down"][0].transpose(1, 0, 2).reshape(H, R0 * RANK)),
        **{f"btab{c}": np.concatenate([gate_b[:, f:f + w], up_b[:, f:f + w]], axis=1)
           for c, (f, w) in enumerate(CHUNKS)},
        "atab": np.concatenate([a_rows, ad_rows], axis=1),
        "la": v["L1_ffn_lora_A"].reshape(N_LORA * RANK, H),
        "lbT": v["L1_ffn_lora_B"].transpose(0, 2, 1).reshape(N_LORA * RANK, H),
        "lw": np.repeat(v["L1_ffn_lora_weights"], RANK).reshape(P, 1),
        "w1T": feat(v["L1_ffn_W"].T),
        "a1": v["L1_cond_A"].reshape(8, 8, KC, P, RANK).transpose(3, 0, 2, 1, 4).reshape(P, 8, KC, P),
        "b1tab": v["L1_cond_B"].reshape(R1, RANK, KC, P).transpose(0, 3, 2, 1).reshape(R1 * P, KC * RANK),
        "bias0": v["L0_ffn_bias"].reshape(1, H),
        "bias1": v["L1_ffn_bias"].reshape(1, H),
        "id0": v["itok_B_2_6"].reshape(1, BATCH),
        "id1": v["itok_B_4_50"].reshape(1, BATCH),
        "consts": constants(),
    }
    arrays = {n: np.ascontiguousarray(a) for n, a in arrays.items()}
    nc = bacc.Bacc("TRN2", target_bir_lowering=False, num_devices=1)
    args = {n: nc.dram_tensor(f"in_{n}", a.shape, mybir.dt.from_np(a.dtype), kind="ExternalInput").ap()
            for n, a in arrays.items()}
    args["btab"] = [args.pop(f"btab{c}") for c in range(NC)]
    args["sb_table"] = nc.dram_tensor("sb_table", (R0 * RANK, H), f32, kind="Internal").ap()
    args["c_table"] = nc.dram_tensor("c_table", (R1 * RANK, H), f32, kind="Internal").ap()
    args["out"] = nc.dram_tensor("out_x", (TOKENS, H), f32, kind="ExternalOutput").ap()
    build_adaln_ffn(nc, **args)
    r = run_bass_kernel_spmd(nc, [{f"in_{n}": a for n, a in arrays.items()}], core_ids=[0])
    return r.results[0]["out_x"].reshape(BATCH, SEQ, H)
```

```python
from contextlib import ExitStack

import numpy as np

import concourse.bass as bass
from concourse import mybir

BATCH, SEQ, H = 128, 32, 512
F = 1376
RANK = 16
R0, R1 = 16, 64
N_LORA = 8
P = 128
TOKENS = BATCH * SEQ
G = TOKENS // P
GB = P // SEQ
KC = H // P
CHUNKS = [(0, 512), (512, 512), (1024, 352)]
BLOCKS = [(f, min(P, F - f)) for f in range(0, F, P)]
NBLK = len(BLOCKS)
CHUNK_BLOCKS = [range(0, 4), range(4, 8), range(8, 11)]
NC = len(CHUNKS)
RING_LAG = [0, -1, 1]
ACT_SLOT = [0, 1, 0]
ACTT_SLOT = [0, 4, 0]
AW = KC * 2 * RANK
ADW = NBLK * RANK
GR = GB * RANK
MW = H + GR
MH = MW // 2
LORA0_SCALE = 0.5
LORA1_SCALE = 2.0
A1_RING = 4
ROWS_RING = 3

f32 = mybir.dt.float32
f32r = mybir.dt.float32r
i32 = mybir.dt.int32
ALU = mybir.AluOpType
ACT = mybir.ActivationFunctionType


def constants():
    p = np.arange(P)
    ident = np.eye(P, dtype=np.float32)
    own = (p[:, None] // SEQ == np.arange(GR)[None, :] // RANK) * np.float32(LORA0_SCALE)
    own_tok = np.concatenate([own, own], axis=1).astype(np.float32)
    own_row = (p[:, None] // (2 * RANK) == p[None, :] // SEQ).astype(np.float32)
    idx = np.zeros((P, 11), np.float32)
    for b in range(GB):
        idx[:, b] = RANK * ((p % GR) // RANK == b)
        idx[:, 5 + b] = RANK * (p // (2 * RANK) == b)
    idx[:, 4] = idx[:, 9] = p % RANK
    idx[:, 10] = p
    return np.concatenate([ident, own_tok, own_row, idx], axis=1).astype(np.float32)


CONST_W = 3 * P + 11


def build_adaln_ffn(nc, xT, x, wgu, signT, wd, bd, btab, atab, la, lbT, lw, w1T, a1, b1tab,
                    bias0, bias1, id0, id1, consts, sb_table, c_table, out):
    ctx = ExitStack()
    with ctx:
        base = (nc.sbuf_base + 31) // 32 * 32
        cursor = [base]

        def place(name, shape, dtype, at=None):
            n = 4 * int(np.prod(shape[1:]))
            n = (n + 31) // 32 * 32
            if at is None:
                at = cursor
            t = nc.alloc_sbuf_tensor_at(name, shape, dtype, offset=at[0])
            at[0] += n
            return t

        w_at = cursor[0]
        w_sb = place("w_sb", [P, 2, 2, KC, F], f32r)
        down_at = [cursor[0]]
        down_sb = place("down_sb", [P, NBLK, 2, MW], f32r)
        down_end = cursor[0]
        xT_raw = place("xT_raw", [P, KC, P], f32)
        xT_sb = place("xT_sb", [P, KC, 2, P], f32r)
        a_raw = place("a_raw", [P, GB, AW + ADW], f32)
        a_sb = place("a_sb", [P, KC, GB, 2, 2 * RANK], f32r)
        t_sum = place("t_sum", [P, 2 * GR], f32)
        t_own = place("t_own", [P, 2, 2, GR], f32)
        tT_sb = place("tT_sb", [P, 2, 2, P], f32r)
        loop_at = [cursor[0]]
        b_raw = place("b_raw", [P, 1024], f32)
        b_sb = [place(f"b_sb{c}", [P, 2 * w], f32r) for c, (_, w) in enumerate(CHUNKS)]
        b_end = cursor[0]
        x_sb = place("x_sb", [P, H], f32)
        x1T_sb = place("x1T_sb", [P, KC, 2, P], f32r)
        act_sb = place("act_sb", [P, 2, 512], f32)
        actT_sb = place("actT_sb", [P, 8, 2, P], f32r)
        td_own = place("td_own", [P, 2, GR], f32)
        tdT_sb = place("tdT_sb", [P, 2, P], f32r)
        t1_sum = place("t1_sum", [P, P], f32)
        t1_sb = place("t1_sb", [P, 2, P], f32r)
        row_raw = place("row_raw", [P, H], f32)
        sbd_sb = place("sbd_sb", [P, H], f32r)
        c_sb = place("c_sb", [P, 2, H], f32r)
        b1_raw = place("b1_raw", [P, GB, KC * RANK], f32)
        b1_sb = place("b1_sb", [P, KC, GB, 2, RANK], f32r)
        loop_end = cursor[0]
        bias_sb = place("bias_sb", [P, 2, H], f32)
        const_sb = place("const_sb", [P, CONST_W], f32)
        idx_rows = place("idx_rows", [P, 2, G], i32)
        idx_feat = place("idx_feat", [P, 2, BATCH], i32)
        now = place("now", [P, 2 * GB + 4], i32)
        now_a, now_b1 = now[:, 0:GB], now[:, GB:2 * GB]
        now_b, now_sb, now_c, zero = (now[:, 2 * GB + n:2 * GB + n + 1] for n in range(4))
        assert cursor[0] <= nc.sbuf_usable_end, (cursor[0], nc.sbuf_usable_end)
        ident = const_sb[:, 0:P]
        own_tok = const_sb[:, P:2 * P]
        own_row = const_sb[:, 2 * P:3 * P]
        idx_c = const_sb[:, 3 * P:CONST_W]

        def in_place(name, shape, at):
            whole = nc.alloc_sbuf_tensor_at(name + "_raw", shape, f32, offset=at[0])
            return whole, place(name + "_lo", shape, f32r, at)

        w_raw = nc.alloc_sbuf_tensor_at("w_raw", [P, 2, 2, KC, F], f32, offset=w_at)
        la_raw, la_lo = in_place("la", [P, H], down_at)
        la_hi = place("la_hi", [P, H], f32r, down_at)
        lb_raw, lb_lo = in_place("lb", [P, H], down_at)
        lb_hi = place("lb_hi", [P, H], f32r, down_at)
        weff_raw, weff_lo = in_place("weff", [P, KC, H], down_at)
        weff_hi = place("weff_hi", [P, KC, H], f32r, down_at)
        a1_raw, a1_lo = in_place("a1", [P, 8, KC, P], down_at)
        a1_hi = place("a1_hi", [P, A1_RING, KC, P], f32r, down_at)
        lw_sb = place("lw_sb", [P, 2], f32, down_at)
        assert down_at[0] <= down_end, (down_at[0], down_end)
        bd_raw, bd_lo = in_place("bd", [P, KC, R0 * RANK], loop_at)
        bd_hi = place("bd_hi", [P, KC, R0 * RANK], f32r, loop_at)
        rows_out = place("rows_out", [P, ROWS_RING, H], f32, loop_at)
        id_raw = place("id_raw", [P, 2, BATCH], i32, loop_at)
        id_f = place("id_f", [P, 2, BATCH], f32, loop_at)
        id_acc = place("id_acc", [P, 2, G], f32, loop_at)
        assert loop_at[0] >= b_end, (loop_at[0], b_end)
        sign_raw = nc.alloc_sbuf_tensor_at("sign_raw", [P, KC, H], f32, offset=loop_at[0])
        sign_sb = place("sign_sb", [P, KC, H], f32r, loop_at)
        wd_raw, wd_lo = in_place("wd", [P, KC, F], loop_at)
        assert loop_at[0] <= loop_end, (loop_at[0], loop_end)
        wd_hi = nc.alloc_sbuf_tensor_at("wd_hi", [P, KC, F], f32r, offset=w_at + 4 * 2 * KC * F)

        def bank(name):
            return ctx.enter_context(nc.psum_tensor(name, [P, 512], f32))

        gate_ps, up_ps = bank("gate_ps"), bank("up_ps")
        y_ps = [bank("y0_ps"), bank("y1_ps")]
        actT_ps, x1T_ps, sum_ps, tT_ps = bank("actT_ps"), bank("x1T_ps"), bank("sum_ps"), bank("tT_ps")
        ring_ps = [y_ps[0], y_ps[1], actT_ps, x1T_ps]

        def sem(name):
            return ctx.enter_context(nc.semaphore(name))

        names = ("const_in", "bias_in", "id_in", "sign_in", "bd_in", "la_in", "lb_in", "w1_in",
                 "sign_done", "wd_hi", "wd_lo", "bd_hi", "bd_lo", "la_hi", "la_lo", "lb_scaled", "lb_hi", "lb_lo",
                 "ids_done", "dve_step", "down_mm", "down_hi", "down_lo", "sbd_mm", "sbd_out", "weff_mm", "weff_sum",
                 "weff_hi", "weff_lo", "a1_hi", "a1_lo", "c_mm", "c_out", "w_hi", "w_lo", "silu_ready")
        S = {n: sem("pro_" + n) for n in names}
        a1_in = [sem(f"pro_a1_in{k}") for k in range(2)]
        wd_in = [sem(f"pro_wd_in{k}") for k in range(KC)]
        wg_in = [sem(f"pro_wg_in{k}") for k in range(KC)]
        wu_in = [sem(f"pro_wu_in{k}") for k in range(KC)]
        rows_free = [sem(f"pro_rows_free{k}") for k in range(ROWS_RING)]
        names = ("xT_in", "xT_hi", "xT_lo", "x_in", "x_biased", "gate_mm", "up_mm", "silu_done", "act_done",
                 "act_tr", "actT_hi", "actT_lo", "down_mm", "a_in", "a_hi", "a_lo", "ad_hi", "ad_lo", "t_mm", "t_added",
                 "t_masked", "t_tr", "tT_hi", "tT_lo", "td_masked", "td_tr", "tdT_hi", "tdT_lo", "y_mm", "x1_done",
                 "x1_tr", "x1T_hi", "x1T_lo", "x1_biased", "b1_in", "b1_hi", "b1_lo", "t1_mm", "t1_added", "t1_masked",
                 "t1_hi", "t1_lo", "c_in", "c_hi", "c_lo", "out_mm", "out_done", "stored", "b_in", "b_hi", "b_lo",
                 "sbd_in", "sbd_hi", "sbd_lo", "idx_a", "idx_b", "idx_sb", "idx_b1", "idx_c")
        L = {n: sem(n) for n in names}
        block = ctx.enter_context(nc.Block())

        def after(engine, semaphore, count):
            if not isinstance(count, int) or count > 0:
                engine.wait_ge(semaphore, count)

        def hi(t):
            return t.bitcast(f32)

        def rows_stored(engine):
            for k in range(ROWS_RING):
                engine.wait_ge(rows_free[k], 16 * len(range(k, 10, ROWS_RING)))

        @block.sync
        def _(sp):
            sp.dma_start(la_raw[:], la).then_inc(S["la_in"], 16)
            sp.dma_start(lb_raw[:], lbT).then_inc(S["lb_in"], 16)
            sp.dma_start(lw_sb[:, 0:1], lw).then_inc(S["lb_in"], 16)
            sp.dma_start(weff_raw[:], w1T).then_inc(S["w1_in"], 16)
            for k in range(2):
                sp.dma_start(a1_raw[:, 4 * k:4 * k + 4], a1[:, 4 * k:4 * k + 4]).then_inc(a1_in[k], 16)
            sp.dma_start(sign_raw[:], signT).then_inc(S["sign_in"], 16)
            sp.dma_start(bd_raw[:], bd).then_inc(S["bd_in"], 16)
            loads = [(wd_raw[:, k, :], wd[:, k, :], wd_in[k]) for k in range(KC)]
            loads += [(w_raw[:, 0, 1, k, :], wgu[:, k, :], wg_in[k]) for k in range(KC)]
            loads += [(xT_raw[:], xT[0:P, :].rearrange("p (k t) -> p k t", k=KC), L["xT_in"])]
            loads += [(w_raw[:, 1, 1, k, :], wgu[:, KC + k, :], wu_in[k]) for k in range(KC)]
            for n in range(10):
                for to, source, arrived in loads[0:2] if n == 0 else loads[n + 1:n + 2]:
                    sp.dma_start(to, source).then_inc(arrived, 16)
                k = n % ROWS_RING
                if n < 8:
                    sp.wait_ge(S["c_out"], n + 1)
                    table, at = c_table, n
                else:
                    sp.wait_ge(S["sbd_out"], n - 7)
                    table, at = sb_table, n - 8
                sp.dma_start(table[at * P:(at + 1) * P, :], rows_out[:, k, :]).then_inc(rows_free[k], 16)
            for to, source, arrived in loads[11:]:
                sp.dma_start(to, source).then_inc(arrived, 16)

            def load_xT(g):
                after(sp, L["xT_lo"], g)
                sp.dma_start(xT_raw[:], xT[bass.ds(g * P, P), :].rearrange("p (k t) -> p k t", k=KC)
                             ).then_inc(L["xT_in"], 16)

            def load_x(g):
                after(sp, L["stored"], 16 * g)
                sp.dma_start(x_sb[:], x[bass.ds(g * P, P), :]).then_inc(L["x_in"], 16)

            def store(g):
                sp.wait_ge(L["out_done"], g + 1)
                sp.dma_start(out[bass.ds(g * P, P), :], x_sb[:]).then_inc(L["stored"], 16)

            load_xT(1)
            sp.wait_ge(S["down_mm"], NBLK)
            rows_stored(sp)
            load_x(0)
            with sp.Fori(1, G - 1) as g:
                load_xT(g + 1)
                store(g - 1)
                load_x(g)
            store(G - 2)
            load_x(G - 1)
            store(G - 1)
            sp.wait_ge(L["stored"], 16 * G)

        @block.gpsimd
        def _(pool):
            pool.dma_start(const_sb[:], consts).then_inc(S["const_in"], 16)
            pool.dma_start(id_raw[:, 0, :], id0.to_broadcast([P, BATCH])).then_inc(S["id_in"], 16)
            pool.dma_start(id_raw[:, 1, :], id1.to_broadcast([P, BATCH])).then_inc(S["id_in"], 16)
            nc.gpsimd.memset(zero, 0).then_inc(S["ids_done"], 1)
            pool.wait_ge(S["ids_done"], 5)

            def gather(dst, index, table, signal):
                nc.gpsimd.indirect_dma_start(
                    out=dst, out_offset=None, in_=table,
                    in_offset=bass.IndirectOffsetOnAxis(ap=index, axis=0)).then_inc(signal, 16)

            def gather_a(g):
                after(pool, L["ad_lo"], g)
                nc.gpsimd.tensor_copy(now_a, idx_feat[:, 0, bass.ds(g * GB, GB)]).then_inc(L["idx_a"], 1)
                pool.wait_ge(L["idx_a"], 1)
                pool.sem_clear(L["idx_a"])
                for b in range(GB):
                    gather(a_raw[:, b, :], now_a[:, b:b + 1], atab, L["a_in"])

            def gather_b(g, c):
                after(pool, L["b_lo"], g * NC + c)
                if c == 0:
                    last = nc.gpsimd.tensor_copy(now_b, idx_rows[:, 0, bass.ds(g, 1)])
                else:
                    last = nc.gpsimd.tensor_tensor(now_b, now_b, zero, ALU.add)
                last.then_inc(L["idx_b"], 1)
                pool.wait_ge(L["idx_b"], 1)
                pool.sem_clear(L["idx_b"])
                gather(b_raw[:, 0:2 * CHUNKS[c][1]], now_b, btab[c], L["b_in"])

            def gather_sbd(g):
                after(pool, L["c_lo"], g)
                nc.gpsimd.tensor_copy(now_sb, idx_rows[:, 0, bass.ds(g, 1)]).then_inc(L["idx_sb"], 1)
                pool.wait_ge(L["idx_sb"], 1)
                pool.sem_clear(L["idx_sb"])
                gather(row_raw[:], now_sb, sb_table, L["sbd_in"])

            def gather_b1(g):
                after(pool, L["b1_lo"], g)
                nc.gpsimd.tensor_copy(now_b1, idx_feat[:, 1, bass.ds(g * GB, GB)]).then_inc(L["idx_b1"], 1)
                pool.wait_ge(L["idx_b1"], 1)
                pool.sem_clear(L["idx_b1"])
                for b in range(GB):
                    gather(b1_raw[:, b, :], now_b1[:, b:b + 1], b1tab, L["b1_in"])

            def gather_c(g):
                pool.wait_ge(L["sbd_lo"], g + 1)
                nc.gpsimd.tensor_copy(now_c, idx_rows[:, 1, bass.ds(g, 1)]).then_inc(L["idx_c"], 1)
                pool.wait_ge(L["idx_c"], 1)
                pool.sem_clear(L["idx_c"])
                gather(row_raw[:], now_c, c_table, L["c_in"])

            def add_bias0(g):
                pool.wait_ge(L["x_in"], 16 * g + 16)
                nc.gpsimd.tensor_tensor(x_sb[:], x_sb[:], bias_sb[:, 0, :], ALU.add).then_inc(L["x_biased"], 1)

            def add_bias1(g):
                pool.wait_ge(L["x1_tr"], g + 1)
                nc.gpsimd.tensor_tensor(x_sb[:], x_sb[:], bias_sb[:, 1, :], ALU.add).then_inc(L["x1_biased"], 1)

            def step(g, prev, nxt):
                if prev is not None:
                    add_bias0(prev)
                elif g is not None:
                    gather_sbd(g)
                    gather_a(nxt)
                if nxt is not None:
                    gather_b(nxt, 0)
                    if prev is not None:
                        gather_a(nxt)
                if g is not None:
                    if prev is not None:
                        gather_sbd(g)
                    gather_b1(g)
                if prev is not None:
                    add_bias1(prev)
                if nxt is not None:
                    gather_b(nxt, 1)
                if g is not None:
                    gather_c(g)
                if nxt is not None:
                    gather_b(nxt, 2)

            gather_a(0)
            pool.dma_start(bias_sb[:, 0, :], bias0.to_broadcast([P, H])).then_inc(S["bias_in"], 16)
            pool.dma_start(bias_sb[:, 1, :], bias1.to_broadcast([P, H])).then_inc(S["bias_in"], 16)
            pool.wait_ge(S["sbd_mm"], 2)
            for c in range(NC):
                gather_b(0, c)
            pool.wait_ge(S["down_mm"], NBLK)
            rows_stored(pool)
            pool.wait_ge(S["bias_in"], 32)
            step(0, None, 1)
            with pool.Fori(1, G - 1) as g:
                step(g, g - 1, g + 1)
            step(G - 1, G - 2, None)
            step(None, G - 1, None)

        @block.scalar
        def _(act):
            def copy(o, i):
                return nc.scalar.copy(o, i)

            def split_xT(g):
                act.wait_ge(L["xT_in"], 16 * g + 16)
                after(act, L["up_mm"], g * NC)
                copy(xT_sb[:, :, 0, :], xT_raw[:]).then_inc(L["xT_hi"], 1)

            def split_a(g):
                act.wait_ge(L["a_in"], 16 * GB * g + 16 * GB)
                after(act, L["t_mm"], g)
                for b in range(GB):
                    last = copy(a_sb[:, :, b, 0, :], a_raw[:, b, 0:AW].rearrange("p (k r) -> p k r", k=KC))
                last.then_inc(L["a_hi"], 1)

            def split_ad(g):
                act.wait_ge(L["a_in"], 16 * GB * g + 16 * GB)
                after(act, L["down_mm"], g * NC)
                for b in range(GB):
                    last = copy(down_sb[:, :, 0, H + b * RANK:H + (b + 1) * RANK],
                                a_raw[:, b, AW:].rearrange("p (n r) -> p n r", n=NBLK))
                last.then_inc(L["ad_hi"], 1)

            def split_b(g, c):
                act.wait_ge(L["b_in"], 16 * (g * NC + c) + 16)
                after(act, L["up_mm"], (g - 1) * NC + c + 1)
                copy(b_sb[c][:], b_raw[:, 0:2 * CHUNKS[c][1]]).then_inc(L["b_hi"], 1)

            def split_sbd(g):
                act.wait_ge(L["sbd_in"], 16 * g + 16)
                after(act, L["y_mm"], g)
                copy(sbd_sb[:], row_raw[:]).then_inc(L["sbd_hi"], 1)

            def split_b1(g):
                act.wait_ge(L["b1_in"], 16 * GB * g + 16 * GB)
                after(act, L["t1_mm"], g)
                for b in range(GB):
                    last = copy(b1_sb[:, :, b, 0, :], b1_raw[:, b, :].rearrange("p (k r) -> p k r", k=KC))
                last.then_inc(L["b1_hi"], 1)

            def split_c(g):
                act.wait_ge(L["c_in"], 16 * g + 16)
                after(act, L["out_mm"], g)
                copy(c_sb[:, 0, :], row_raw[:]).then_inc(L["c_hi"], 1)

            def silu(g, c):
                w = CHUNKS[c][1]
                act.wait_ge(L["gate_mm"], g * NC + c + 1)
                after(act, L["act_tr"], g * NC + RING_LAG[c])
                nc.scalar.activation(act_sb[:, ACT_SLOT[c], 0:w], gate_ps[:, 0:w], ACT.Silu).then_inc(L["silu_done"], 1)

            def split_actT(g, c):
                n = len(CHUNK_BLOCKS[c])
                act.wait_ge(L["act_tr"], g * NC + c + 1)
                after(act, L["down_mm"], g * NC + RING_LAG[c])
                copy(actT_sb[:, ACTT_SLOT[c]:ACTT_SLOT[c] + n, 0, :],
                     actT_ps[:, 0:n * P].rearrange("p (n t) -> p n t", n=n)).then_inc(L["actT_hi"], 1)

            def split_t(g):
                act.wait_ge(L["t_tr"], g + 1)
                after(act, L["up_mm"], g * NC)
                copy(tT_sb[:, 0, :, :], tT_ps[:, 0:2 * P].rearrange("p (u t) -> p u t", u=2)).then_inc(L["tT_hi"], 1)

            def split_td(g):
                act.wait_ge(L["td_tr"], g + 1)
                after(act, L["y_mm"], g)
                copy(tdT_sb[:, 0, :], tT_ps[:, 0:P]).then_inc(L["tdT_hi"], 1)

            def split_x1(g):
                act.wait_ge(L["x1_tr"], g + 1)
                after(act, L["t1_mm"], g)
                copy(x1T_sb[:, :, 0, :], x1T_ps[:].rearrange("p (k t) -> p k t", k=KC)).then_inc(L["x1T_hi"], 1)

            def split_up(c):
                f, w = CHUNKS[c]
                for k in range(KC):
                    act.wait_ge(wu_in[k], 16)
                    copy(w_sb[:, 1, 0, k, f:f + w], w_raw[:, 1, 1, k, f:f + w]).then_inc(S["w_hi"], 1)

            def split_t1(g):
                act.wait_ge(L["t1_masked"], g + 1)
                after(act, L["out_mm"], g)
                copy(t1_sb[:, 0, :], t1_sum[:]).then_inc(L["t1_hi"], 1)

            def step(g, prev, nxt):
                if g is not None:
                    split_ad(g)
                    silu(g, 0)
                    if prev is None:
                        split_up(2)
                        split_b(0, 2)
                if prev is not None:
                    split_td(prev)
                if g is not None:
                    split_sbd(g)
                    silu(g, 1)
                    split_actT(g, 0)
                if prev is not None:
                    split_x1(prev)
                if nxt is not None:
                    split_b(nxt, 0)
                if prev is not None:
                    split_t1(prev)
                if g is not None:
                    if prev is not None:
                        split_b1(g)
                    silu(g, 2)
                    split_actT(g, 1)
                if nxt is not None:
                    split_a(nxt)
                    split_xT(nxt)
                    split_b(nxt, 1)
                if g is not None:
                    split_actT(g, 2)
                if nxt is not None:
                    split_t(nxt)
                if g is not None:
                    if prev is None:
                        split_b1(g)
                    split_c(g)
                if nxt is not None:
                    split_b(nxt, 2)

            act.wait_ge(S["la_in"], 16)
            copy(la_hi[:], la_raw[:]).then_inc(S["la_hi"], 1)
            act.wait_ge(S["lb_scaled"], 1)
            copy(lb_hi[:], lb_raw[:]).then_inc(S["lb_hi"], 1)

            def split_a1(n):
                act.wait_ge(a1_in[n // 4], 16)
                after(act, S["c_mm"], n - A1_RING + 1)
                copy(a1_hi[:, n % A1_RING, :, :], a1_raw[:, n, :, :]).then_inc(S["a1_hi"], 1)

            def split_wd(k):
                act.wait_ge(wd_in[k], 16)
                copy(wd_hi[:, k, :], wd_raw[:, k, :]).then_inc(S["wd_hi"], 1)

            def rows_slot(n):
                after(act, rows_free[n % ROWS_RING], 16 * (n // ROWS_RING))
                return rows_out[:, n % ROWS_RING, :]

            for k in range(KC):
                act.wait_ge(S["weff_sum"], k + 1)
                copy(weff_hi[:, k, :], weff_raw[:, k, :]).then_inc(S["weff_hi"], 1)
                if k == 2:
                    split_a1(0)
            for n in range(1, A1_RING):
                split_a1(n)
            for n in range(8):
                act.wait_ge(S["c_mm"], n + 1)
                copy(rows_slot(n), ring_ps[(KC + n) % 4][:]).then_inc(S["c_out"], 1)
                if n + A1_RING < 8:
                    split_a1(n + A1_RING)
                if n == 2:
                    act.wait_ge(S["sign_in"], 16)
                    nc.scalar.activation(sign_sb[:], sign_raw[:], ACT.Sign).then_inc(S["sign_done"], 1)
                if n == 3:
                    act.wait_ge(S["bd_in"], 16)
                    copy(bd_hi[:], bd_raw[:]).then_inc(S["bd_hi"], 1)
                if 3 <= n < 3 + KC:
                    split_wd(n - 3)
            for n in range(2):
                act.wait_ge(S["sbd_mm"], n + 1)
                copy(rows_slot(8 + n), ring_ps[(KC + 8 + n) % 4][:]).then_inc(S["sbd_out"], 1)
            for n, (_, m) in enumerate(BLOCKS):
                act.wait_ge(S["down_mm"], n + 1)
                copy(down_sb[0:m, n, 0, 0:H], ring_ps[(KC + 10 + n) % 4][0:m, :]).then_inc(S["down_hi"], 1)
                if n < KC:
                    act.wait_ge(wg_in[n], 16)
                    copy(w_sb[:, 0, 0, n, :], w_raw[:, 0, 1, n, :]).then_inc(S["w_hi"], 1)
                if n == 4:
                    split_xT(0)
                    split_a(0)
                if n == 5:
                    split_b(0, 0)
                if n == 7:
                    act.wait_ge(S["const_in"], 16)
                    nc.scalar.activation(tT_ps[:, 2 * P:2 * P + 1], ident[:, 0:1], ACT.Silu
                                         ).then_inc(S["silu_ready"], 1)
                if n == 9:
                    split_t(0)
            split_up(0)
            rows_stored(act)
            split_b(0, 1)
            split_up(1)
            step(0, None, 1)
            with act.Fori(1, G - 1) as g:
                step(g, g - 1, g + 1)
            step(G - 1, G - 2, None)
            step(None, G - 1, None)

        @block.vector
        def _(dve):
            def lo(o, whole, high):
                return nc.vector.tensor_tensor(o, whole, hi(high), ALU.subtract)

            steps = [0]

            def link(instruction):
                steps[0] += 1
                instruction.then_inc(S["dve_step"], 1)
                dve.wait_ge(S["dve_step"], steps[0])

            def split_xT(g):
                dve.wait_ge(L["xT_hi"], g + 1)
                lo(xT_sb[:, :, 1, :], xT_raw[:], xT_sb[:, :, 0, :]).then_inc(L["xT_lo"], 1)

            def split_a(g):
                dve.wait_ge(L["a_hi"], g + 1)
                for b in range(GB):
                    last = lo(a_sb[:, :, b, 1, :], a_raw[:, b, 0:AW].rearrange("p (k r) -> p k r", k=KC),
                              a_sb[:, :, b, 0, :])
                last.then_inc(L["a_lo"], 1)

            def split_ad(g):
                dve.wait_ge(L["ad_hi"], g + 1)
                for b in range(GB):
                    cols = slice(H + b * RANK, H + (b + 1) * RANK)
                    last = lo(down_sb[:, :, 1, cols], a_raw[:, b, AW:].rearrange("p (n r) -> p n r", n=NBLK),
                              down_sb[:, :, 0, cols])
                last.then_inc(L["ad_lo"], 1)

            def split_b(g, c):
                dve.wait_ge(L["b_hi"], g * NC + c + 1)
                lo(b_sb[c][GR:, :], b_raw[GR:, 0:2 * CHUNKS[c][1]], b_sb[c][GR:, :]).then_inc(L["b_lo"], 1)

            def split_sbd(g):
                dve.wait_ge(L["sbd_hi"], g + 1)
                lo(sbd_sb[GR:, :], row_raw[GR:, :], sbd_sb[GR:, :]).then_inc(L["sbd_lo"], 1)

            def split_b1(g):
                dve.wait_ge(L["b1_hi"], g + 1)
                for b in range(GB):
                    last = lo(b1_sb[:, :, b, 1, :], b1_raw[:, b, :].rearrange("p (k r) -> p k r", k=KC),
                              b1_sb[:, :, b, 0, :])
                last.then_inc(L["b1_lo"], 1)

            def split_c(g):
                dve.wait_ge(L["c_hi"], g + 1)
                lo(c_sb[:, 1, :], row_raw[:], c_sb[:, 0, :]).then_inc(L["c_lo"], 1)

            def gated(g, c):
                w = CHUNKS[c][1]
                dve.wait_ge(L["up_mm"], g * NC + c + 1)
                dve.wait_ge(L["silu_done"], g * NC + c + 1)
                a = act_sb[:, ACT_SLOT[c], 0:w]
                nc.vector.tensor_tensor(a, a, up_ps[:, 0:w], ALU.mult).then_inc(L["act_done"], 1)

            def split_actT(g, c):
                n, at = len(CHUNK_BLOCKS[c]), ACTT_SLOT[c]
                dve.wait_ge(L["actT_hi"], g * NC + c + 1)
                lo(actT_sb[:, at:at + n, 1, :], actT_ps[:, 0:n * P].rearrange("p (n t) -> p n t", n=n),
                   actT_sb[:, at:at + n, 0, :]).then_inc(L["actT_lo"], 1)

            def own_t(g):
                dve.wait_ge(L["t_mm"], g + 1)
                s = sum_ps[:, 0:4 * GR].rearrange("p (b h u r) -> p h u b r", b=GB, h=2, u=2)
                t = t_sum[:].rearrange("p (u b r) -> p u b r", u=2, b=GB)
                nc.vector.tensor_copy(t, s[:, 0]).then_inc(L["t_added"], 1)
                dve.wait_ge(L["t_added"], 2 * g + 1)
                nc.vector.tensor_tensor(t, t, s[:, 1], ALU.add).then_inc(L["t_added"], 1)
                dve.wait_ge(L["t_added"], 2 * g + 2)
                after(dve, L["t_tr"], g)
                for d in range(2):
                    last = nc.vector.tensor_tensor(t_own[:, :, d, :], t_sum[:].rearrange("p (u r) -> p u r", u=2),
                                                   own_tok.rearrange("p (u r) -> p u r", u=2), ALU.mult)
                last.then_inc(L["t_masked"], 1)

            def split_t(g):
                dve.wait_ge(L["tT_hi"], g + 1)
                lo(tT_sb[:, 1, :, :], tT_ps[:, 0:2 * P].rearrange("p (u t) -> p u t", u=2), tT_sb[:, 0, :, :]
                   ).then_inc(L["tT_lo"], 1)

            def own_td(g):
                dve.wait_ge(L["down_mm"], g * NC + NC)
                after(dve, L["td_tr"], g)
                for d in range(2):
                    last = nc.vector.tensor_tensor(td_own[:, d, :], y_ps[1][:, H - MH:MH], own_tok[:, 0:GR], ALU.mult)
                last.then_inc(L["td_masked"], 1)

            def split_td(g):
                dve.wait_ge(L["tdT_hi"], g + 1)
                lo(tdT_sb[:, 1, :], tT_ps[:, 0:P], tdT_sb[:, 0, :]).then_inc(L["tdT_lo"], 1)

            def add_y(g):
                dve.wait_ge(L["y_mm"], g + 1)
                dve.wait_ge(L["x_biased"], g + 1)
                nc.vector.tensor_tensor(x_sb[:, 0:MH], x_sb[:, 0:MH], y_ps[0][:, 0:MH], ALU.add)
                nc.vector.tensor_tensor(x_sb[:, MH:H], x_sb[:, MH:H], y_ps[1][:, 0:H - MH],
                                        ALU.add).then_inc(L["x1_done"], 1)

            def split_x1(g):
                dve.wait_ge(L["x1T_hi"], g + 1)
                lo(x1T_sb[:, :, 1, :], x1T_ps[:].rearrange("p (k t) -> p k t", k=KC), x1T_sb[:, :, 0, :]
                   ).then_inc(L["x1T_lo"], 1)

            def split_up(c):
                f, w = CHUNKS[c]
                for k in range(KC):
                    dve.wait_ge(S["w_hi"], KC + c * KC + k + 1)
                    lo(w_sb[:, 1, 1, k, f:f + w], w_raw[:, 1, 1, k, f:f + w], w_sb[:, 1, 0, k, f:f + w]
                       ).then_inc(S["w_lo"], 1)

            def own_t1(g):
                dve.wait_ge(L["t1_mm"], g + 1)
                nc.vector.tensor_copy(t1_sum[:], sum_ps[:, 0:P]).then_inc(L["t1_added"], 1)
                dve.wait_ge(L["t1_added"], 2 * g + 1)
                nc.vector.tensor_tensor(t1_sum[:], t1_sum[:], sum_ps[:, P:2 * P], ALU.add).then_inc(L["t1_added"], 1)
                dve.wait_ge(L["t1_added"], 2 * g + 2)
                nc.vector.tensor_tensor(t1_sum[:], t1_sum[:], own_row, ALU.mult).then_inc(L["t1_masked"], 1)
                dve.wait_ge(L["t1_hi"], g + 1)
                lo(t1_sb[:, 1, :], t1_sum[:], t1_sb[:, 0, :]).then_inc(L["t1_lo"], 1)

            def add_out(g):
                dve.wait_ge(L["out_mm"], g + 1)
                dve.wait_ge(L["x1_biased"], g + 1)
                nc.vector.tensor_tensor(x_sb[:], x_sb[:], sum_ps[:], ALU.add).then_inc(L["out_done"], 1)

            def step(g, prev, nxt):
                if prev is not None:
                    own_td(prev)
                if g is not None:
                    split_ad(g)
                if prev is not None:
                    split_td(prev)
                if g is not None:
                    gated(g, 0)
                if prev is not None:
                    add_y(prev)
                elif g is not None:
                    split_up(2)
                    split_b(0, 2)
                if g is not None:
                    split_sbd(g)
                    split_actT(g, 0)
                if prev is not None:
                    split_x1(prev)
                if g is not None:
                    gated(g, 1)
                if nxt is not None:
                    split_b(nxt, 0)
                if prev is not None:
                    own_t1(prev)
                if g is not None:
                    if prev is not None:
                        split_b1(g)
                    split_actT(g, 1)
                if nxt is not None:
                    split_a(nxt)
                if g is not None:
                    gated(g, 2)
                if nxt is not None:
                    split_xT(nxt)
                if prev is not None:
                    add_out(prev)
                if nxt is not None:
                    split_b(nxt, 1)
                if g is not None:
                    split_actT(g, 2)
                if nxt is not None:
                    own_t(nxt)
                    split_t(nxt)
                if g is not None:
                    if prev is None:
                        split_b1(g)
                    split_c(g)
                if nxt is not None:
                    split_b(nxt, 2)

            dve.wait_ge(S["lb_in"], 32)
            link(nc.vector.tensor_scalar(lw_sb[:, 1:2], lw_sb[:, 0:1], LORA1_SCALE, None, ALU.mult))
            nc.vector.tensor_scalar(lb_raw[:], lb_raw[:], lw_sb[:, 1:2], None, ALU.mult).then_inc(S["lb_scaled"], 1)
            dve.wait_ge(S["la_hi"], 1)
            lo(la_lo[:], la_raw[:], la_hi[:]).then_inc(S["la_lo"], 1)
            dve.wait_ge(S["lb_hi"], 1)
            lo(lb_lo[:], lb_raw[:], lb_hi[:]).then_inc(S["lb_lo"], 1)
            def split_a1(n):
                dve.wait_ge(S["a1_hi"], n + 1)
                lo(a1_lo[:, n, :, :], a1_raw[:, n, :, :], a1_hi[:, n % A1_RING, :, :]).then_inc(S["a1_lo"], 1)

            dve.wait_ge(S["w1_in"], 16)
            for k in range(KC + 1):
                if k < KC:
                    dve.wait_ge(S["weff_mm"], k + 1)
                    nc.vector.tensor_tensor(weff_raw[:, k, :], weff_raw[:, k, :], ring_ps[k][:], ALU.add
                                            ).then_inc(S["weff_sum"], 1)
                if k > 0:
                    dve.wait_ge(S["weff_hi"], k)
                    lo(weff_lo[:, k - 1, :], weff_raw[:, k - 1, :], weff_hi[:, k - 1, :]).then_inc(S["weff_lo"], 1)
                if k == KC - 1:
                    split_a1(0)

            for n in range(1, A1_RING):
                split_a1(n)
            dve.wait_ge(S["id_in"], 32)
            dve.wait_ge(S["const_in"], 16)
            for n, count in enumerate((R0, R1)):
                link(nc.vector.tensor_scalar(id_f[:, n, :], id_raw[:, n, :], float(count - 1), 0.0, ALU.min, ALU.max))
                nc.vector.tensor_scalar(idx_feat[:, n, :], id_f[:, n, :], float(P), idx_c[:, 10:11],
                                        ALU.mult, ALU.add).then_inc(S["ids_done"], 1)
                own = id_f[:, n, :].rearrange("p (g b) -> p b g", b=GB)
                link(nc.vector.tensor_scalar(id_acc[:, n, :], own[:, 0, :], idx_c[:, 5 * n:5 * n + 1],
                                             idx_c[:, 5 * n + 4:5 * n + 5], ALU.mult, ALU.add))
                for b in range(1, GB):
                    to = idx_rows if b == GB - 1 else id_acc
                    last = nc.vector.scalar_tensor_tensor(to[:, n, :], own[:, b, :], idx_c[:, 5 * n + b:5 * n + b + 1],
                                                          id_acc[:, n, :], ALU.mult, ALU.add)
                    if b < GB - 1:
                        link(last)
                last.then_inc(S["ids_done"], 1)
            for n in range(A1_RING, 8):
                split_a1(n)
            dve.wait_ge(S["bd_hi"], 1)
            lo(bd_lo[:], bd_raw[:], bd_hi[:]).then_inc(S["bd_lo"], 1)
            for k in range(KC):
                dve.wait_ge(S["wd_hi"], k + 1)
                lo(wd_lo[:, k, :], wd_raw[:, k, :], wd_hi[:, k, :]).then_inc(S["wd_lo"], 1)
            for n, (_, m) in enumerate(BLOCKS):
                dve.wait_ge(S["down_hi"], n + 1)
                lo(down_sb[0:m, n, 1, 0:H], ring_ps[(KC + 10 + n) % 4][0:m, :], down_sb[0:m, n, 0, 0:H]
                   ).then_inc(S["down_lo"], 1)
                if n < KC:
                    dve.wait_ge(S["w_hi"], n + 1)
                    lo(w_sb[:, 0, 1, n, :], w_raw[:, 0, 1, n, :], w_sb[:, 0, 0, n, :]).then_inc(S["w_lo"], 1)
                if n == 4:
                    split_xT(0)
                    split_a(0)
                if n == 5:
                    split_b(0, 0)
                if n == 8:
                    own_t(0)
                if n == 9:
                    split_t(0)
            split_up(0)
            split_b(0, 1)
            split_up(1)
            step(0, None, 1)
            with dve.Fori(1, G - 1) as g:
                step(g, g - 1, g + 1)
            step(G - 1, G - 2, None)
            step(None, G - 1, None)

        @block.tensor
        def _(pe):
            def product(o, terms, signal, start=True, stop=True, check=True):
                for n, (w, m) in enumerate(terms):
                    last = nc.tensor.matmul(o, w, m, start=start and n == 0, stop=stop and n == len(terms) - 1,
                                            skip_group_check=not check)
                return last.then_inc(signal, 1) if signal is not None else last

            THREE = ((0, 0), (0, 1), (1, 0))

            def t_product(g):
                pe.wait_ge(L["xT_lo"], g + 1)
                pe.wait_ge(L["a_lo"], g + 1)
                after(pe, L["t_masked"], g)
                after(pe, L["t1_masked"], g - 1)
                after(pe, L["out_done"], g - 1)
                product(sum_ps[:, 0:4 * GR], [(xT_sb[:, k, h, :], a_sb[:, k, :, :, :].rearrange("p b h r -> p (b h r)"))
                                              for k in range(KC) for h in range(2)], L["t_mm"])

            def t_transpose(g):
                pe.wait_ge(L["t_masked"], g + 1)
                after(pe, L["tdT_lo"], g - 1)
                for u in range(2):
                    last = nc.tensor.transpose(tT_ps[:, u * P:(u + 1) * P], t_own[:, u, :, :].rearrange("p d r -> p (d r)"), ident)
                last.then_inc(L["t_tr"], 1)

            def gate_up(g, c, u):
                f, w = CHUNKS[c]
                o = (gate_ps, up_ps)[u][:, 0:w]
                if c == 0 and u == 0:
                    pe.wait_ge(L["xT_lo"], g + 1)
                if isinstance(g, int) and g == 0:
                    pe.wait_ge(S["w_lo"], KC + u * (c + 1) * KC)
                after(pe, L[("silu_done", "act_done")[u]], g * NC + c)
                for n, (k, a, b) in enumerate((k, a, b) for k in range(KC) for a, b in THREE):
                    nc.tensor.matmul(o, xT_sb[:, k, a, :], w_sb[:, u, b, k, f:f + w], start=n == 0, stop=False)
                if c == 0 and u == 0:
                    pe.wait_ge(L["tT_lo"], g + 1)
                if u == 0:
                    pe.wait_ge(L["b_lo"], g * NC + c + 1)
                for a in range(2):
                    last = nc.tensor.matmul(o, tT_sb[:, a, u, :], b_sb[c][:, u * w:(u + 1) * w], start=False,
                                            stop=a == 1)
                last.then_inc(L[("gate_mm", "up_mm")[u]], 1)

            def act_transpose(g, c):
                f, w = CHUNKS[c]
                pe.wait_ge(L["act_done"], g * NC + c + 1)
                after(pe, L["actT_lo"], g * NC + c)
                if isinstance(g, int) and g == 0 and c == 0:
                    pe.wait_ge(S["down_lo"], NBLK)
                for n, blk in enumerate(CHUNK_BLOCKS[c]):
                    m = BLOCKS[blk][1]
                    last = nc.tensor.transpose(actT_ps[0:m, n * P:(n + 1) * P],
                                               act_sb[:, ACT_SLOT[c], n * P:n * P + m], ident)
                last.then_inc(L["act_tr"], 1)

            def down(g, c):
                pe.wait_ge(L["actT_lo"], g * NC + c + 1)
                if c == 0:
                    pe.wait_ge(L["ad_lo"], g + 1)
                    after(pe, L["x1_done"], g)
                for n, blk in enumerate(CHUNK_BLOCKS[c]):
                    m = BLOCKS[blk][1]
                    for a, b in THREE:
                        for half in range(2):
                            last = nc.tensor.matmul(
                                y_ps[half][:, 0:MH], actT_sb[0:m, ACTT_SLOT[c] + n, a, :],
                                down_sb[0:m, blk, b, half * MH:(half + 1) * MH],
                                start=blk == 0 and (a, b) == (0, 0), stop=blk == NBLK - 1 and (a, b) == (1, 0))
                last.then_inc(L["down_mm"], 1)

            def td_transpose(g):
                pe.wait_ge(L["td_masked"], g + 1)
                if isinstance(g, int) and g == G - 1:
                    pe.wait_ge(L["tT_lo"], G)
                else:
                    pe.wait_ge(L["tT_lo"], g + 2)
                nc.tensor.transpose(tT_ps[:, 0:P], td_own[:].rearrange("p d r -> p (d r)"), ident
                                    ).then_inc(L["td_tr"], 1)

            def down_lora(g):
                pe.wait_ge(L["tdT_lo"], g + 1)
                pe.wait_ge(L["sbd_lo"], g + 1)
                for a in range(2):
                    for half, (c0, c1) in enumerate(((0, MH), (MH, H))):
                        last = nc.tensor.matmul(y_ps[half][:, 0:c1 - c0], tdT_sb[:, a, :], sbd_sb[:, c0:c1],
                                                start=False, stop=a == 1, skip_group_check=True)
                last.then_inc(L["y_mm"], 1)

            def x1_transpose(g):
                pe.wait_ge(L["x1_done"], g + 1)
                after(pe, L["x1T_lo"], g)
                for k in range(KC):
                    last = nc.tensor.transpose(x1T_ps[:, k * P:(k + 1) * P], x_sb[:, k * P:(k + 1) * P], ident)
                last.then_inc(L["x1_tr"], 1)

            def t1_product(g):
                pe.wait_ge(L["x1T_lo"], g + 1)
                pe.wait_ge(L["b1_lo"], g + 1)
                if isinstance(g, int) and g == G - 1:
                    pe.wait_ge(L["t_masked"], G)
                else:
                    pe.wait_ge(L["t_masked"], g + 2)
                after(pe, L["out_done"], g)
                product(sum_ps[:, 0:2 * P], [(b1_sb[:, k, :, :, :].rearrange("p b h r -> p (b h r)"),
                                              x1T_sb[:, k, :, :].rearrange("p h t -> p (h t)"))
                                             for k in range(KC)], L["t1_mm"])

            def out_product(g):
                pe.wait_ge(L["t1_lo"], g + 1)
                pe.wait_ge(L["c_lo"], g + 1)
                product(sum_ps[:], [(t1_sb[:, a, :], c_sb[:, b, :]) for a, b in THREE], L["out_mm"])

            def step(g, prev, nxt):
                if g is not None:
                    gate_up(g, 0, 0)
                if prev is not None:
                    td_transpose(prev)
                if g is not None:
                    gate_up(g, 0, 1)
                if prev is not None:
                    down_lora(prev)
                if g is not None:
                    gate_up(g, 1, 0)
                    act_transpose(g, 0)
                if prev is not None:
                    x1_transpose(prev)
                if g is not None:
                    gate_up(g, 1, 1)
                if prev is not None:
                    t1_product(prev)
                if g is not None:
                    gate_up(g, 2, 0)
                    act_transpose(g, 1)
                    gate_up(g, 2, 1)
                if prev is not None:
                    out_product(prev)
                if g is not None:
                    down(g, 0)
                if nxt is not None:
                    t_product(nxt)
                if g is not None:
                    act_transpose(g, 2)
                    down(g, 1)
                if nxt is not None:
                    t_transpose(nxt)
                if g is not None:
                    down(g, 2)

            pe.wait_ge(S["la_lo"], 1)
            pe.wait_ge(S["lb_lo"], 1)
            la_parts, lb_parts = (la_hi, la_lo), (lb_hi, lb_lo)
            for k in range(KC):
                product(ring_ps[k][:], [(la_parts[a][:, k * P:(k + 1) * P], lb_parts[b][:]) for a, b in THREE],
                        S["weff_mm"])
            weff = (weff_hi, weff_lo)
            for n in range(8):
                pe.wait_ge(S["a1_lo"], n + 1)
                after(pe, S["c_out"], n - 3)
                a1_parts = (a1_hi[:, n % A1_RING, :, :], a1_lo[:, n, :, :])
                for k in range(KC):
                    pe.wait_ge(S["weff_lo"], k + 1)
                    product(ring_ps[(KC + n) % 4][:], [(a1_parts[a][:, k, :], weff[b][:, k, :]) for a, b in THREE],
                            S["c_mm"] if k == KC - 1 else None, start=k == 0, stop=k == KC - 1)
            pe.wait_ge(S["sign_done"], 1)
            pe.wait_ge(S["bd_lo"], 1)
            for n in range(2):
                pe.wait_ge(S["c_out"], 5 + n)
                product(ring_ps[(KC + 8 + n) % 4][:], [(half[:, k, n * P:(n + 1) * P], sign_sb[:, k, :])
                                                       for k in range(KC) for half in (bd_hi, bd_lo)], S["sbd_mm"])
            pe.wait_ge(S["wd_lo"], KC)
            for n, (f, m) in enumerate(BLOCKS):
                if n < 2:
                    pe.wait_ge(S["c_out"], 7 + n)
                elif n < 4:
                    pe.wait_ge(S["sbd_out"], n - 1)
                else:
                    pe.wait_ge(S["down_lo"], n - 3)
                product(ring_ps[(KC + 10 + n) % 4][0:m, :], [(half[:, k, f:f + m], sign_sb[:, k, :])
                                                             for k in range(KC) for half in (wd_hi, wd_lo)],
                        S["down_mm"])
                if n == 8:
                    t_product(0)
                if n == 9:
                    pe.wait_ge(S["silu_ready"], 1)
                    t_transpose(0)
            step(0, None, 1)
            with pe.Fori(1, G - 1) as g:
                step(g, g - 1, g + 1)
            step(G - 1, G - 2, None)
            step(None, G - 1, None)


def kernel(**inputs):
    import concourse.bacc as bacc
    from concourse.bass_utils import run_bass_kernel_spmd

    v = {n: np.ascontiguousarray(a) for n, a in inputs.items()}
    x = v["x"].reshape(TOKENS, H)
    feat = lambda a: a.reshape(KC, P, -1).transpose(1, 0, 2)
    gate_b = v["L0_cond_B_gate"][0].transpose(0, 2, 1).reshape(R0 * RANK, F)
    up_b = v["L0_cond_B_up"][0].transpose(0, 2, 1).reshape(R0 * RANK, F)
    a_rows = np.concatenate([v["L0_cond_A_gate"][0][:, None], v["L0_cond_A_up"][0][:, None]], axis=1)
    a_rows = a_rows.reshape(R0, 2, RANK, KC, P).transpose(0, 4, 3, 1, 2).reshape(R0 * P, AW)
    ad_rows = np.zeros((R0, RANK, NBLK * P), np.float32)
    ad_rows[:, :, 0:F] = v["L0_cond_A_down"][0]
    ad_rows = ad_rows.reshape(R0, RANK, NBLK, P).transpose(0, 3, 2, 1).reshape(R0 * P, ADW)
    arrays = {
        "xT": x.reshape(G, P, KC, P).transpose(0, 3, 2, 1).reshape(G * P, H),
        "x": x,
        "wgu": np.stack([feat(v["L0_cond_W_gate"].T), feat(v["L0_cond_W_up"].T)], axis=1).reshape(P, 2 * KC, F),
        "signT": feat(v["L0_ffn_weight"].T),
        "wd": feat(v["L0_cond_W_down"]),
        "bd": feat(v["L0_cond_B_down"][0].transpose(1, 0, 2).reshape(H, R0 * RANK)),
        **{f"btab{c}": np.concatenate([gate_b[:, f:f + w], up_b[:, f:f + w]], axis=1)
           for c, (f, w) in enumerate(CHUNKS)},
        "atab": np.concatenate([a_rows, ad_rows], axis=1),
        "la": v["L1_ffn_lora_A"].reshape(N_LORA * RANK, H),
        "lbT": v["L1_ffn_lora_B"].transpose(0, 2, 1).reshape(N_LORA * RANK, H),
        "lw": np.repeat(v["L1_ffn_lora_weights"], RANK).reshape(P, 1),
        "w1T": feat(v["L1_ffn_W"].T),
        "a1": v["L1_cond_A"].reshape(8, 8, KC, P, RANK).transpose(3, 0, 2, 1, 4).reshape(P, 8, KC, P),
        "b1tab": v["L1_cond_B"].reshape(R1, RANK, KC, P).transpose(0, 3, 2, 1).reshape(R1 * P, KC * RANK),
        "bias0": v["L0_ffn_bias"].reshape(1, H),
        "bias1": v["L1_ffn_bias"].reshape(1, H),
        "id0": v["itok_B_2_6"].reshape(1, BATCH),
        "id1": v["itok_B_4_50"].reshape(1, BATCH),
        "consts": constants(),
    }
    arrays = {n: np.ascontiguousarray(a) for n, a in arrays.items()}
    nc = bacc.Bacc("TRN2", target_bir_lowering=False, num_devices=1)
    args = {n: nc.dram_tensor(f"in_{n}", a.shape, mybir.dt.from_np(a.dtype), kind="ExternalInput").ap()
            for n, a in arrays.items()}
    args["btab"] = [args.pop(f"btab{c}") for c in range(NC)]
    args["sb_table"] = nc.dram_tensor("sb_table", (R0 * RANK, H), f32, kind="Internal").ap()
    args["c_table"] = nc.dram_tensor("c_table", (R1 * RANK, H), f32, kind="Internal").ap()
    args["out"] = nc.dram_tensor("out_x", (TOKENS, H), f32, kind="ExternalOutput").ap()
    build_adaln_ffn(nc, **args)
    r = run_bass_kernel_spmd(nc, [{f"in_{n}": a for n, a in arrays.items()}], core_ids=[0])
    return r.results[0]["out_x"].reshape(BATCH, SEQ, H)
```
